# Optimizing a Trainium2 kernel written in Bass

```python
import numpy as np
import jax
import jax.numpy as jnp

def _softmax(x, axis=-1):
    return jax.nn.softmax(x, axis=axis)

def _gelu(x):
    return jax.nn.gelu(x, approximate=True)

def _silu(x):
    return jax.nn.silu(x)

def _sigmoid(x):
    return jax.nn.sigmoid(x)

def _layernorm(x, axis=-1, eps=1e-05):
    m = jnp.mean(x, axis=axis, keepdims=True)
    v = jnp.var(x, axis=axis, keepdims=True)
    return (x - m) / jnp.sqrt(v + eps)

def _scatter_add(tgt, idx, src, axis=0):
    return tgt.at[idx].add(src)

def _segment_sum(src, seg, n):
    return jax.ops.segment_sum(src, seg, n)
kernel_name = 'mk_decoder_preln_d1_seqx_r4_d7a339'

def setup_inputs(seed: int=0):
    np.random.seed(seed)
    _w = jnp.asarray

    def _rec_inputs():
        import jax
        import jax.numpy as jnp
        _rk = jax.random.key(seed)
        x = 0.0003765 + 1 * jax.random.normal(jax.random.fold_in(_rk, 1), (8, 256, 512), jnp.float32)
        _lenS = 256 - jax.random.randint(jax.random.fold_in(_rk, 7), (8,), 0, max(1, 256 // 4) + 1, jnp.int32)
        _lenS2 = 256 - jax.random.randint(jax.random.fold_in(_rk, 8), (8,), 0, max(1, 256 // 4) + 1, jnp.int32)
        _ctx_2048P = jax.random.normal(jax.random.fold_in(_rk, 11), (8, 16, 512), jnp.float32)
        _ctx_2048c = jax.random.dirichlet(jax.random.fold_in(_rk, 511), 0.3 * jnp.ones((16,), jnp.float32), (8, 256))
        _ctx_2048t = jnp.einsum('bsk,bkd->bsd', _ctx_2048c, _ctx_2048P)
        _ctx_2048t = _ctx_2048t * jax.lax.rsqrt(jnp.mean(jnp.square(_ctx_2048t)) + 1e-12) * 0.953939
        ctx_2048 = -0.000292821 + 1.00034 * (_ctx_2048t + 0.3 * jax.random.normal(jax.random.fold_in(_rk, 611), (8, 256, 512), jnp.float32))
        return (x, ctx_2048)
    x, ctx_2048 = _rec_inputs()

    def _L0_attn_setup():
        import jax, jax.numpy as jnp
        import numpy as np
        HID = 512
        HEADS = 16
        HD = HID // HEADS
        EPS = 1e-06

        def _heads(x, b, s):
            return x.reshape(b, s, HEADS, HD).transpose(0, 2, 1, 3)
        key = jax.random.key(seed)
        ks = jax.random.split(key, 9)
        s = 1.0 / np.sqrt(HID)
        return {'hidden_states': jax.random.normal(ks[0], (4, 1024, HID), jnp.float32), 'q_w': jax.random.normal(ks[1], (HID, HID), jnp.float32) * s, 'q_b': jnp.zeros((HID,), jnp.float32), 'k_w': jax.random.normal(ks[2], (HID, HID), jnp.float32) * s, 'k_b': jnp.zeros((HID,), jnp.float32), 'v_w': jax.random.normal(ks[3], (HID, HID), jnp.float32) * s, 'v_b': jnp.zeros((HID,), jnp.float32), 'o_w': jax.random.normal(ks[4], (HID, HID), jnp.float32) * s, 'o_b': jnp.zeros((HID,), jnp.float32)}
    _L0_attn_all = _L0_attn_setup()
    _L0_attn_in = {k: v for k, v in _L0_attn_all.items() if k in ('q_w', 'q_b', 'k_w', 'k_b', 'v_w', 'v_b', 'o_w', 'o_b')}
    del _L0_attn_all

    def _L0_xattn_setup():
        import jax, jax.numpy as jnp
        import numpy as np
        key = jax.random.key(seed)
        k1, k2, k3, k4, k5 = jax.random.split(key, 5)
        B, D_MODEL, L = (2, 256, 512)
        HEAD_DIM = 8
        H = D_MODEL // HEAD_DIM
        return {'k': jax.random.normal(k1, (B, D_MODEL, L), dtype=jnp.float32), 'v': jax.random.normal(k2, (B, D_MODEL, L), dtype=jnp.float32), 'q': jax.random.normal(k3, (B, D_MODEL, L), dtype=jnp.float32), 'ssm_kernel': jax.random.normal(k4, (H, L), dtype=jnp.float32), 'D': jax.random.normal(k5, (H,), dtype=jnp.float32), 'head_dim': HEAD_DIM}
    _L0_xattn_all = _L0_xattn_setup()
    _L0_xattn_in = {k: v for k, v in _L0_xattn_all.items() if k in ('ssm_kernel', 'D')}
    del _L0_xattn_all

    def _L0_ffn_setup():
        import jax, jax.numpy as jnp
        import numpy as np
        NUM_EXPERTS = 16
        TOP_K = 4
        N_GROUP = 4
        TOPK_GROUP = 2
        SCALING = 2.5

        def _route(x, gate_weight, expert_bias):
            logits = x @ gate_weight.T
            scores = jax.nn.sigmoid(logits)
            biased = scores + expert_bias[None, :]
            T = x.shape[0]
            gsz = NUM_EXPERTS // N_GROUP
            grp = biased.reshape(T, N_GROUP, gsz)
            top2, _ = jax.lax.top_k(grp, 2)
            group_scores = top2.sum(-1)
            _, gidx = jax.lax.top_k(group_scores, TOPK_GROUP)
            gmask = jax.nn.one_hot(gidx, N_GROUP, dtype=scores.dtype).sum(1)
            emask = jnp.repeat(gmask, gsz, axis=1)
            masked = jnp.where(emask > 0, biased, -jnp.inf)
            _, sel = jax.lax.top_k(masked, TOP_K)
            w = jnp.take_along_axis(scores, sel, axis=1)
            w = w / (w.sum(-1, keepdims=True) + 1e-20)
            return (w * SCALING, sel)

        def _moe(x, w, sel, gate_proj, up_proj, down_proj):
            cw = (jax.nn.one_hot(sel, NUM_EXPERTS, dtype=x.dtype) * w[..., None]).sum(1)

            def body(acc, inp):
                g, u, d, we = inp
                y = jax.nn.silu(x @ g.T) * (x @ u.T) @ d.T
                return (acc + we[:, None] * y, None)
            out, _ = jax.lax.scan(body, jnp.zeros_like(x), (gate_proj, up_proj, down_proj, cw.T))
            return out
        key = jax.random.key(seed)
        ks = jax.random.split(key, 9)
        B, S, H, I = (2, 256, 512, 256)
        w = lambda k, shape: jax.random.normal(k, shape, jnp.float32) * 0.02
        return {'hidden_states': jax.random.normal(ks[0], (B, S, H), jnp.float32), 'gate_weight': w(ks[1], (NUM_EXPERTS, H)), 'expert_bias': jnp.zeros((NUM_EXPERTS,), jnp.float32), 'gate_proj': w(ks[2], (NUM_EXPERTS, I, H)), 'up_proj': w(ks[3], (NUM_EXPERTS, I, H)), 'down_proj': w(ks[4], (NUM_EXPERTS, H, I)), 'shared_gate': w(ks[5], (I, H)), 'shared_up': w(ks[6], (I, H)), 'shared_down': w(ks[7], (H, I))}
    _L0_ffn_all = _L0_ffn_setup()
    _L0_ffn_in = {k: v for k, v in _L0_ffn_all.items() if k in ('gate_weight', 'expert_bias', 'gate_proj', 'up_proj', 'down_proj', 'shared_gate', 'shared_up', 'shared_down')}
    del _L0_ffn_all
    return {'x': x, 'ctx_2048': ctx_2048, 'L0_attn_q_w': _L0_attn_in['q_w'], 'L0_attn_q_b': _L0_attn_in['q_b'], 'L0_attn_k_w': _L0_attn_in['k_w'], 'L0_attn_k_b': _L0_attn_in['k_b'], 'L0_attn_v_w': _L0_attn_in['v_w'], 'L0_attn_v_b': _L0_attn_in['v_b'], 'L0_attn_o_w': _L0_attn_in['o_w'], 'L0_attn_o_b': _L0_attn_in['o_b'], 'L0_xattn_ssm_kernel': _L0_xattn_in['ssm_kernel'], 'L0_xattn_D': _L0_xattn_in['D'], 'L0_ffn_gate_weight': _L0_ffn_in['gate_weight'], 'L0_ffn_expert_bias': _L0_ffn_in['expert_bias'], 'L0_ffn_gate_proj': _L0_ffn_in['gate_proj'], 'L0_ffn_up_proj': _L0_ffn_in['up_proj'], 'L0_ffn_down_proj': _L0_ffn_in['down_proj'], 'L0_ffn_shared_gate': _L0_ffn_in['shared_gate'], 'L0_ffn_shared_up': _L0_ffn_in['shared_up'], 'L0_ffn_shared_down': _L0_ffn_in['shared_down']}

def reference(x, ctx_2048, L0_attn_q_w, L0_attn_q_b, L0_attn_k_w, L0_attn_k_b, L0_attn_v_w, L0_attn_v_b, L0_attn_o_w, L0_attn_o_b, L0_xattn_ssm_kernel, L0_xattn_D, L0_ffn_gate_weight, L0_ffn_expert_bias, L0_ffn_gate_proj, L0_ffn_up_proj, L0_ffn_down_proj, L0_ffn_shared_gate, L0_ffn_shared_up, L0_ffn_shared_down):
    import jax
    import jax.numpy as jnp

    def _L0_attn_ref(hidden_states, q_w, q_b, k_w, k_b, v_w, v_b, o_w, o_b):
        import jax, jax.numpy as jnp
        import numpy as np
        HID = 512
        HEADS = 16
        HD = HID // HEADS
        EPS = 1e-06

        def _heads(x, b, s):
            return x.reshape(b, s, HEADS, HD).transpose(0, 2, 1, 3)
        b, s, _ = hidden_states.shape
        q = _heads(hidden_states @ q_w.T + q_b, b, s)
        k = _heads(hidden_states @ k_w.T + k_b, b, s)
        v = _heads(hidden_states @ v_w.T + v_b, b, s)
        qp = jax.nn.elu(q) + 1.0
        kp = jax.nn.elu(k) + 1.0
        kv = jnp.einsum('bhsd,bhse->bhde', kp, v)
        z = jnp.einsum('bhsd,bhd->bhs', qp, kp.sum(axis=2))[..., None]
        attn = jnp.einsum('bhsd,bhde->bhse', qp, kv) / (z + EPS)
        out = attn.transpose(0, 2, 1, 3).reshape(b, s, HID)
        return out @ o_w.T + o_b

    def _L0_xattn_ref(k, v, q, ssm_kernel, D, head_dim):
        import jax, jax.numpy as jnp
        import numpy as np
        B, HD, L = k.shape
        H = HD // head_dim
        fft_size = 2 * L
        k_ = k.reshape(B, H, head_dim, L)
        v_ = v.reshape(B, H, head_dim, L)
        q_ = q.reshape(B, H, head_dim, L)
        kv = jnp.einsum('bhil,bhjl->bijhl', k_, v_)
        kv_f = jnp.fft.rfft(kv, n=fft_size)
        kernel_f = jnp.fft.rfft(ssm_kernel, n=fft_size)
        y = jnp.fft.irfft(kv_f * kernel_f, n=fft_size)[..., :L]
        out = y + kv * D[None, None, None, :, None]
        out = jnp.einsum('bijhl,bhil->bjhl', out, q_)
        out = jnp.transpose(out, (0, 2, 1, 3)).reshape(B, H * head_dim, L)
        return out.astype(k.dtype)

    def _L0_ffn_ref(hidden_states, gate_weight, expert_bias, gate_proj, up_proj, down_proj, shared_gate, shared_up, shared_down):
        import jax, jax.numpy as jnp
        import numpy as np
        NUM_EXPERTS = 16
        TOP_K = 4
        N_GROUP = 4
        TOPK_GROUP = 2
        SCALING = 2.5

        def _route(x, gate_weight, expert_bias):
            logits = x @ gate_weight.T
            scores = jax.nn.sigmoid(logits)
            biased = scores + expert_bias[None, :]
            T = x.shape[0]
            gsz = NUM_EXPERTS // N_GROUP
            grp = biased.reshape(T, N_GROUP, gsz)
            top2, _ = jax.lax.top_k(grp, 2)
            group_scores = top2.sum(-1)
            _, gidx = jax.lax.top_k(group_scores, TOPK_GROUP)
            gmask = jax.nn.one_hot(gidx, N_GROUP, dtype=scores.dtype).sum(1)
            emask = jnp.repeat(gmask, gsz, axis=1)
            masked = jnp.where(emask > 0, biased, -jnp.inf)
            _, sel = jax.lax.top_k(masked, TOP_K)
            w = jnp.take_along_axis(scores, sel, axis=1)
            w = w / (w.sum(-1, keepdims=True) + 1e-20)
            return (w * SCALING, sel)

        def _moe(x, w, sel, gate_proj, up_proj, down_proj):
            cw = (jax.nn.one_hot(sel, NUM_EXPERTS, dtype=x.dtype) * w[..., None]).sum(1)

            def body(acc, inp):
                g, u, d, we = inp
                y = jax.nn.silu(x @ g.T) * (x @ u.T) @ d.T
                return (acc + we[:, None] * y, None)
            out, _ = jax.lax.scan(body, jnp.zeros_like(x), (gate_proj, up_proj, down_proj, cw.T))
            return out
        B, S, H = hidden_states.shape
        x = hidden_states.reshape(-1, H)
        w, sel = _route(x, gate_weight, expert_bias)
        out = _moe(x, w, sel, gate_proj, up_proj, down_proj)
        shared = jax.nn.silu(x @ shared_gate.T) * (x @ shared_up.T) @ shared_down.T
        return (out + shared).reshape(B, S, H)
    x = x + _L0_attn_ref(_layernorm(x, axis=-1), L0_attn_q_w, L0_attn_q_b, L0_attn_k_w, L0_attn_k_b, L0_attn_v_w, L0_attn_v_b, L0_attn_o_w, L0_attn_o_b)
    x = x + _L0_xattn_ref(ctx_2048, ctx_2048, _layernorm(x, axis=-1), L0_xattn_ssm_kernel, L0_xattn_D, 8)
    x = x + _L0_ffn_ref(_layernorm(x, axis=-1), L0_ffn_gate_weight, L0_ffn_expert_bias, L0_ffn_gate_proj, L0_ffn_up_proj, L0_ffn_down_proj, L0_ffn_shared_gate, L0_ffn_shared_up, L0_ffn_shared_down)
    return x

_drawn_inputs = setup_inputs


def setup_inputs(seed=0):
    import zlib

    import numpy as np

    out = dict(_drawn_inputs(seed))
    spreads = {'L0_attn_q_b': (0.0, 2.0),
     'L0_attn_k_b': (0.0, 2.0),
     'L0_attn_v_b': (0.0, 0.1),
     'L0_attn_o_b': (0.0, 0.1),
     'L0_ffn_expert_bias': (0.0, 0.8)}
    factors = {'L0_attn_q_w': 8.0,
     'L0_attn_k_w': 3.405,
     'L0_ffn_gate_weight': 8.0,
     'L0_ffn_gate_proj': 8.0,
     'L0_ffn_up_proj': 8.0,
     'L0_ffn_down_proj': 8.0,
     'L0_ffn_shared_gate': 8.0,
     'L0_ffn_shared_up': 8.0,
     'L0_ffn_shared_down': 8.0}
    for name, (base, spread) in spreads.items():
        noise = np.random.default_rng([zlib.crc32(name.encode()), seed]).standard_normal(out[name].shape)
        drawn = base * np.exp(spread * noise) if base else spread * noise
        out[name] = jnp.asarray(drawn.astype(out[name].dtype))
    for name, factor in factors.items():
        out[name] = (out[name] * factor).astype(out[name].dtype)
    return out
```

```python
from contextlib import ExitStack

import numpy as np

import concourse.bass as bass
from concourse import mybir

F32 = mybir.dt.float32
F32R = mybir.dt.float32r
I32 = mybir.dt.int32
U32 = mybir.dt.uint32
ALU = mybir.AluOpType
ACT = mybir.ActivationFunctionType
AX_X = mybir.AxisListType.X

P = 128
B, S, D = 8, 256, 512
NT = B * S // P
TPB = S // P
DC = D // P
HEADS, HD = 16, 32
CH, CD = 32, 8
NPAIR = CD * (CD + 1) // 2
GPD = P // HD
NE, I_FF = 16, 256
IC = I_FF // P
TOPK = 4
SLOT_T = 2
SLOT = SLOT_T * P
NSLOT = B * S * TOPK // SLOT + NE - 1
NSLOT += NSLOT % 2
NFULL = B * S * TOPK // SLOT // 2
NROW = NSLOT * SLOT
NCOL = NROW // P
LN_EPS = 1e-5
ATT_EPS = 1e-6
BIG = 3.0e38
KPAD = P - 1 + D


def decoder_program(nc, x, ctx2, qwT, kwT, vwT, owT, q_b, k_b, v_b, o_b, ssm, dskip, gateT, ebias,
                    gu_w, dn_w, c_ident, c_block, c_head, c_lt4, c_tri, c_free, c_slotk,
                    c_tok, out):
    with ExitStack() as ctx:
        def sb(name, shape, dt=F32):
            return ctx.enter_context(nc.sbuf_tensor(name, shape, dt))

        def sem(name):
            return ctx.enter_context(nc.semaphore(name))

        kpad_d = nc.dram_tensor("kpad_d", (CH, KPAD + 1), F32).ap()
        xs_d = nc.dram_tensor("xs_d", (B * S + SLOT, D), F32).ap()

        PS = ctx.enter_context(nc.psum_tensor("PS", [P, 8, 512], F32))

        X = sb("X", [P, NT, D])
        ident = sb("ident", [P, P])
        nhalf = sb("nhalf", [P, TPB])
        Tz = [sb(f"Tz{k}", [P, D]) for k in range(2)]
        C2 = [sb(f"C2{k}", [P, DC * B, 2 * CD]) for k in range(2)]
        QY = sb("QY", [P, DC, B, S])
        wstage = QY[:].rearrange("p c b s -> p (c b s)").rearrange("p (w c n) -> p w c n", w=4, c=DC)
        st1 = ExitStack()

        def sb1(name, shape, dt=F32):
            return st1.enter_context(nc.sbuf_tensor(name, shape, dt))
        WH = sb1("WH", [P, 4, DC, D], F32R)
        WL = sb1("WL", [P, 4, DC, D], F32R)
        qb = sb1("qb", [P, DC])
        kb = sb1("kb", [P, D])
        vb = sb1("vb", [P, D])
        ob = sb1("ob", [P, D])
        block = sb1("block", [P, P])
        headm = sb1("headm", [P, DC, HEADS])
        stt = [sb1(f"bn_stat{i}", [P, TPB, 6]) for i in range(2)]
        mv = [sb1(f"mean_var{i}", [P, TPB, 2]) for i in range(2)]
        ve = [sb1(f"var_eps{i}", [P, TPB]) for i in range(2)]
        rs = [sb1(f"rstd{i}", [P, TPB]) for i in range(2)]
        xn = [sb1(f"xn{i}", [P, TPB, D]) for i in range(2)]
        xTh = sb1("xTh", [P, DC, S], F32R)
        xTl = sb1("xTl", [P, DC, S], F32R)
        qE = sb1("qE", [P, DC, S])
        qR = sb1("qR", [P, DC, S])
        qpT = sb1("qpT", [P, DC, S])
        kt = sb1("kt", [P, TPB, D])
        kE = sb1("kE", [P, TPB, D])
        nqb = sb1("nqb", [P, DC])
        kp = sb1("kp", [P, TPB, D])
        v1 = sb1("v1", [P, TPB, DC, P + 1])
        KV = sb1("KV", [P, DC, P])
        KS = sb1("KS", [P, DC, HEADS])
        dn = sb1("dn", [P, TPB * HEADS])
        rd = sb1("rd", [P, TPB * HEADS])
        at = sb1("at", [P, TPB, D])
        aTh = sb1("aTh", [P, DC, S], F32R)
        aTl = sb1("aTl", [P, DC, S], F32R)
        xo = xn[1]

        kpad = sb1("kpad", [CH, KPAD + 1])
        dsk = sb1("dsk", [CH, 1])
        ssm_in = sem("ssm_in")
        kpad_zero, kpad_done, kpad_out = sem("kpad_zero"), sem("kpad_done"), sem("kpad_out")
        tc_in = [sem(f"tc_in{k}") for k in range(2)]
        consts_in = sem("consts_in")
        x_in = sem("x_in")
        x_ready = sem("x_ready")
        w_in = [sem(f"w_in{i}") for i in range(4)]
        memsets = sem("memsets")
        w_hi = sem("w_hi")
        w_lo = sem("w_lo")
        wo_lo = sem("wo_lo")
        bn = [sem(f"ln{i}_bn") for i in range(2)]
        mvs = [sem(f"ln{i}_mv") for i in range(2)]
        ves = [sem(f"ln{i}_ve") for i in range(2)]
        rss = [sem(f"ln{i}_rstd") for i in range(2)]
        xns = [sem(f"ln{i}_xn") for i in range(2)]
        trs = [sem(f"ln{i}_transposed") for i in range(2)]
        xT_hi, xT_lo = sem("xT_hi"), sem("xT_lo")
        nqb_done, km_done = sem("nqb_done"), sem("km_done")
        q_ps, q_neg, q_act, qp_done = sem("q_ps"), sem("q_neg"), sem("q_act"), sem("qp_done")
        k_ps, kt_done, k_act, kp_done = sem("k_ps"), sem("kt_done"), sem("k_act"), sem("kp_done")
        v_ps, v_done = sem("v_ps"), sem("v_done")
        kv_ps, kv_done = sem("kv_ps"), sem("kv_done")
        att_ps, dn_done, rd_done, at_done = sem("att_ps"), sem("dn_done"), sem("rd_done"), sem("at_done")
        aT_ps, aT_hi, aT_lo = sem("aT_ps"), sem("aT_hi"), sem("aT_lo")
        o_ps, xo_done, x1_done = sem("o_ps"), sem("xo_done"), sem("x1_done")
        qy_done = sem("qy_done")

        block1 = nc.Block()
        block_ = block1.__enter__()

        def bcast_rows(v):
            return bass.AP(tensor=v.tensor, offset=0, ap=[[0, P], [1, D]])

        passed = {}

        def wait_apart(eng, semaphore, value):
            if eng.engine not in passed:
                passed[eng.engine] = sem(f"passed_{len(passed)}")
            eng.wait_ge(semaphore, value)
            eng.sem_inc(passed[eng.engine], 1)

        def load_head(sp, h, k):
            sp.dma_start(Tz[k][:], bass.AP(tensor=kpad_d.tensor, offset=h * (KPAD + 1), ap=[[1, P], [1, D]])
                         ).then_inc(tc_in[k], 16)
            sp.dma_start(C2[k][:], ctx2[h].rearrange("p c b j -> p (c b) j")).then_inc(tc_in[k], 16)

        @block_.sync
        def _(sp):
            sp.dma_start(ident[:], c_ident).then_inc(consts_in, 16)
            for i, w in enumerate((qwT, kwT)):
                sp.dma_start(wstage[:, i], w.rearrange("(c p) n -> p c n", p=P)).then_inc(w_in[i], 16)
            sp.dma_start(qb[:], q_b).then_inc(consts_in, 16)
            sp.dma_start(kb[:], bcast_rows(k_b)).then_inc(consts_in, 16)
            sp.dma_start(vb[:], bcast_rows(v_b)).then_inc(consts_in, 16)
            sp.dma_start(ob[:], bcast_rows(o_b)).then_inc(consts_in, 16)
            sp.dma_start(block[:], c_block).then_inc(consts_in, 16)
            sp.dma_start(headm[:], c_head).then_inc(consts_in, 16)
            for i, w in enumerate((vwT, owT)):
                sp.dma_start(wstage[:, 2 + i], w.rearrange("(c p) n -> p c n", p=P)).then_inc(w_in[2 + i], 16)
            sp.wait_ge(kpad_zero, 1)
            sp.dma_start(kpad[:, P - 1:KPAD], ssm).then_inc(ssm_in, 16)
            sp.dma_start(dsk[:], dskip).then_inc(ssm_in, 16)
            sp.wait_ge(kpad_done, 1)
            sp.dma_start(kpad_d, kpad[:]).then_inc(kpad_out, 16)
            sp.wait_ge(kpad_out, 16)
            for k in range(2):
                load_head(sp, k, k)
        def rstd(pool, ln, b):
            wait_apart(pool, mvs[ln], TPB * (b + 1))
            nc.gpsimd.tensor_scalar(ve[ln][:], mv[ln][:, :, 1], LN_EPS, None, ALU.add).then_inc(ves[ln], 1)
            pool.wait_ge(ves[ln], b + 1)
            nc.gpsimd.tensor_tensor(rs[ln][:], ve[ln][:], nhalf[:], ALU.pow).then_inc(rss[ln], 1)

        @block_.gpsimd
        def _(pool):
            nc.gpsimd.memset(kpad[:], 0.0).then_inc(kpad_zero, 1)
            nc.gpsimd.memset(nhalf[:], -0.5).then_inc(memsets, 1)
            nc.gpsimd.memset(v1[:, :, :, P:P + 1], 1.0).then_inc(memsets, 1)
            for b in range(B):
                pool.dma_start(X[:, TPB * b:TPB * (b + 1)], x[b].rearrange("(t p) n -> p t n", p=P)).then_inc(x_in, 16)
                pool.wait_ge(x_in, 16 * (b + 1))
                pool.sem_inc(x_ready, 1)
                if b == 0:
                    pool.wait_ge(memsets, 2)
                    rstd(pool, 0, 0)
            pool.wait_ge(w_in[3], 16)
            pool.wait_ge(w_hi, 4)
            nc.gpsimd.tensor_tensor(WL[:, 3], wstage[:, 3], WH[:, 3].bitcast(F32), ALU.subtract).then_inc(wo_lo, 1)
            rstd(pool, 0, 1)
            with pool.Fori(1, B - 1) as b:
                rstd(pool, 0, b + 1)
                rstd(pool, 1, b - 1)
            rstd(pool, 1, B - 2)
            rstd(pool, 1, B - 1)

        @block_.scalar
        def _(act):
            def split_hi(i):
                act.wait_ge(w_in[i], 16)
                act.activation(WH[:, i], wstage[:, i], ACT.Copy).then_inc(w_hi, 1)

            def x_hi(b):
                for t in range(TPB):
                    act.wait_ge(trs[0], TPB * b + t + 1)
                    act.activation(xTh[:, :, t * P:(t + 1) * P], PS[:, 6 + t].rearrange("p (c n) -> p c n", c=DC),
                                   ACT.Copy).then_inc(xT_hi, 1)

            def q_evac(b):
                for c in range(DC):
                    act.wait_ge(q_ps, DC * b + 2 * (c // 2) + 2)
                    ps = PS[:, 4 + c // 2, (c % 2) * S:(c % 2 + 1) * S]
                    act.activation(qE[:, c], ps, ACT.Relu, scale=-1.0, bias=nqb[:, c:c + 1]).then_inc(q_neg, 1)
                    act.activation(qR[:, c], ps, ACT.Relu, bias=qb[:, c:c + 1]).then_inc(q_act, 1)
                act.wait_ge(q_neg, DC * (b + 1))
                act.activation(qE[:], qE[:], ACT.Exp, scale=-1.0).then_inc(q_act, 1)

            def k_evac(b):
                for t in range(TPB):
                    act.wait_ge(km_done, TPB * b + t + 1)
                    act.activation(kE[:, t], kE[:, t], ACT.Exp).then_inc(k_act, 1)

            def a_hi(b):
                for t in range(TPB):
                    act.wait_ge(aT_ps, TPB * b + t + 1)
                    act.activation(aTh[:, :, t * P:(t + 1) * P], PS[:, 6 + t].rearrange("p (c n) -> p c n", c=DC),
                                   ACT.Copy).then_inc(aT_hi, 1)

            def qy_evac(b):
                for t in range(TPB):
                    wait_apart(act, trs[1], TPB * b + t + 1)
                    act.activation(QY[:, :, b, t * P:(t + 1) * P], PS[:, 6 + t].rearrange("p (c n) -> p c n", c=DC),
                                   ACT.Copy).then_inc(qy_done, 1)

            def step(b, first=False, last=False):
                q_evac(b)
                k_evac(b)
                if not first:
                    a_hi(b - 1)
                if not last:
                    x_hi(b + 1)
                if not first:
                    qy_evac(b - 1)

            for i in range(3):
                split_hi(i)
            act.wait_ge(nqb_done, 1)
            x_hi(0)
            split_hi(3)
            step(0, first=True)
            step(1)
            with act.Fori(2, B - 1) as b:
                step(b)
            step(B - 1, last=True)
            a_hi(B - 1)
            qy_evac(B - 1)

        @block_.vector
        def _(dve):
            def ln_stats(ln, b):
                for t in range(TPB):
                    if ln == 0:
                        wait_apart(dve, x_ready, b + 1)
                    else:
                        wait_apart(dve, x1_done, TPB * b + t + 1)
                    dve.bn_stats(stt[ln][:, t], X[:, TPB * b + t]).then_inc(bn[ln], 1)
                    wait_apart(dve, bn[ln], TPB * b + t + 1)
                    dve.bn_aggr(mv[ln][:, t], stt[ln][:, t]).then_inc(mvs[ln], 1)

            def ln_norm(ln, b):
                dve.wait_ge(rss[ln], b + 1)
                dve.wait_ge(trs[ln], TPB * b)
                for t in range(TPB):
                    dve.tensor_scalar(xn[ln][:, t], X[:, TPB * b + t], mv[ln][:, t, 0:1], rs[ln][:, t:t + 1],
                                      ALU.subtract, ALU.mult).then_inc(xns[ln], 1)

            def x_lo(b):
                for t in range(TPB):
                    dve.wait_ge(xT_hi, TPB * b + t + 1)
                    dve.tensor_tensor(xTl[:, :, t * P:(t + 1) * P], PS[:, 6 + t].rearrange("p (c n) -> p c n", c=DC),
                                      xTh[:, :, t * P:(t + 1) * P].bitcast(F32), ALU.subtract).then_inc(xT_lo, 1)

            def qp(b):
                dve.wait_ge(q_act, (DC + 1) * (b + 1))
                dve.tensor_tensor(qpT[:], qE[:], qR[:], ALU.add).then_inc(qp_done, 1)

            def k_bias(b):
                for t in range(TPB):
                    dve.wait_ge(k_ps, TPB * b + t + 1)
                    dve.tensor_tensor(kt[:, t], PS[:, t], kb[:], ALU.add).then_inc(kt_done, 1)
                for t in range(TPB):
                    dve.wait_ge(kt_done, TPB * b + t + 1)
                    dve.tensor_scalar(kE[:, t], kt[:, t], 0.0, None, ALU.min).then_inc(km_done, 1)

            def k_phi(b):
                for t in range(TPB):
                    dve.wait_ge(k_act, TPB * b + t + 1)
                    dve.scalar_tensor_tensor(out=kp[:, t], in0=kt[:, t], scalar=0.0, in1=kE[:, t], op0=ALU.max,
                                             op1=ALU.add).then_inc(kp_done, 1)

            def v_bias(b):
                for t in range(TPB):
                    dve.wait_ge(v_ps, TPB * b + t + 1)
                    dve.tensor_tensor(v1[:, t, :, 0:P], PS[:, 2 + t].rearrange("p (c n) -> p c n", c=DC),
                                      vb[:].rearrange("p (c n) -> p c n", c=DC), ALU.add).then_inc(v_done, 1)

            def kv_mask(b):
                dve.wait_ge(kv_ps, b + 1)
                for h in range(2):
                    ps = PS[:, 4 + h, 0:2 * (P + 1)].rearrange("p (c n) -> p c n", c=2)
                    dve.tensor_tensor(KV[:, 2 * h:2 * h + 2], ps[:, :, 0:P],
                                      block[:].unsqueeze(1).broadcast_to([P, 2, P]), ALU.mult).then_inc(kv_done, 1)
                    dve.tensor_tensor(KS[:, 2 * h:2 * h + 2], ps[:, :, P:P + 1].broadcast_to([P, 2, HEADS]),
                                      headm[:, 2 * h:2 * h + 2], ALU.mult).then_inc(kv_done, 1)

            def att_norm(b):
                dve.wait_ge(att_ps, TPB * (b + 1))
                dve.tensor_scalar(dn[:], PS[:, 2, 0:TPB * HEADS], ATT_EPS, None, ALU.add).then_inc(dn_done, 1)
                dve.wait_ge(dn_done, b + 1)
                dve.reciprocal(rd[:], dn[:]).then_inc(rd_done, 1)
                dve.wait_ge(rd_done, b + 1)
                for t in range(TPB):
                    dve.tensor_tensor(at[:, t].rearrange("p (h n) -> p h n", n=HD),
                                      PS[:, t].rearrange("p (h n) -> p h n", n=HD),
                                      rd[:, t * HEADS:(t + 1) * HEADS].unsqueeze(2).broadcast_to([P, HEADS, HD]),
                                      ALU.mult).then_inc(at_done, 1)

            def a_lo(b):
                for t in range(TPB):
                    dve.wait_ge(aT_hi, TPB * b + t + 1)
                    dve.tensor_tensor(aTl[:, :, t * P:(t + 1) * P], PS[:, 6 + t].rearrange("p (c n) -> p c n", c=DC),
                                      aTh[:, :, t * P:(t + 1) * P].bitcast(F32), ALU.subtract).then_inc(aT_lo, 1)

            def x_add(b):
                for t in range(TPB):
                    dve.wait_ge(o_ps, TPB * b + t + 1)
                    dve.tensor_tensor(xo[:, t], PS[:, 6 + t], ob[:], ALU.add).then_inc(xo_done, 1)
                for t in range(TPB):
                    dve.wait_ge(xo_done, TPB * b + t + 1)
                    dve.tensor_tensor(X[:, TPB * b + t], X[:, TPB * b + t], xo[:, t], ALU.add).then_inc(x1_done, 1)

            def step(b, first=False, last=False):
                if not first:
                    att_norm(b - 1)
                if not last:
                    ln_stats(0, b + 1)
                qp(b)
                if not last:
                    ln_norm(0, b + 1)
                k_bias(b)
                if not first:
                    a_lo(b - 1)
                k_phi(b)
                v_bias(b)
                if not first:
                    x_add(b - 1)
                kv_mask(b)
                if not first:
                    ln_stats(1, b - 1)
                if not last:
                    x_lo(b + 1)
                if not first:
                    ln_norm(1, b - 1)

            ln_stats(0, 0)
            ln_norm(0, 0)
            dve.wait_ge(consts_in, 16 * 7)
            dve.tensor_scalar(nqb[:], qb[:], -1.0, None, ALU.mult).then_inc(nqb_done, 1)
            dve.wait_ge(ssm_in, 32)
            dve.tensor_tensor(kpad[:, P - 1:P], kpad[:, P - 1:P], dsk[:], ALU.add).then_inc(kpad_done, 1)
            for i in range(3):
                dve.wait_ge(w_hi, i + 1)
                dve.tensor_tensor(WL[:, i], wstage[:, i], WH[:, i].bitcast(F32), ALU.subtract).then_inc(w_lo, 1)
            x_lo(0)
            dve.wait_ge(memsets, 2)
            step(0, first=True)
            step(1)
            with dve.Fori(2, B - 1) as b:
                step(b)
            step(B - 1, last=True)
            att_norm(B - 1)
            a_lo(B - 1)
            x_add(B - 1)
            ln_stats(1, B - 1)
            ln_norm(1, B - 1)

        @block_.tensor
        def _(pe):
            def transpose_tiles(src, banks, done):
                for t in range(TPB):
                    for c in range(DC):
                        last = pe.transpose(PS[:, banks + t, c * P:(c + 1) * P], src[:, t, c * P:(c + 1) * P], ident[:])
                    last.then_inc(done, 1)

            def three_pass(out_, lh, ll, rh, rl, first, last):
                pe.matmul(out_, lh, rh, start=first, stop=False)
                pe.matmul(out_, lh, rl, start=False, stop=False)
                return pe.matmul(out_, ll, rh, start=False, stop=last)

            def t1(b):
                pe.wait_ge(xns[0], TPB * (b + 1))
                if not (isinstance(b, int) and b <= 1):
                    pe.wait_ge(xo_done, TPB * (b - 1))
                transpose_tiles(xn[0], 6, trs[0])

            def qproj(b):
                pe.wait_ge(xT_hi, TPB * (b + 1))
                pe.wait_ge(xT_lo, TPB * (b + 1))
                pe.wait_ge(kv_done, 4 * b)
                for c in range(DC):
                    o = PS[:, 4 + c // 2, (c % 2) * S:(c % 2 + 1) * S]
                    for hc in range(DC):
                        w = (0, hc, slice(c * P, (c + 1) * P))
                        mm = three_pass(o, WH[(slice(None),) + w], WL[(slice(None),) + w], xTh[:, hc], xTl[:, hc],
                                        hc == 0, hc == DC - 1)
                    mm.then_inc(q_ps, 1)

            def token_proj(i, srch, srcl, bank, done):
                for t in range(TPB):
                    for c in range(DC):
                        ts = slice(t * P, (t + 1) * P)
                        mm = three_pass(PS[:, bank + t], srch[:, c, ts], srcl[:, c, ts], WH[:, i, c], WL[:, i, c],
                                        c == 0, c == DC - 1)
                    mm.then_inc(done, 1)

            def att_t(b):
                pe.wait_ge(at_done, TPB * (b + 1))
                pe.wait_ge(qy_done, TPB * b)
                transpose_tiles(at, 6, aT_ps)

            def oproj(b):
                pe.wait_ge(aT_hi, TPB * (b + 1))
                pe.wait_ge(aT_lo, TPB * (b + 1))
                token_proj(3, aTh, aTl, 6, o_ps)

            def kv(b):
                pe.wait_ge(kp_done, TPB * (b + 1))
                pe.wait_ge(v_done, TPB * (b + 1))
                pe.wait_ge(q_act, (DC + 1) * (b + 1))
                for c in range(DC):
                    o = PS[:, 4 + c // 2, (c % 2) * (P + 1):(c % 2 + 1) * (P + 1)]
                    for t in range(TPB):
                        mm = pe.matmul(o, kp[:, t, c * P:(c + 1) * P], v1[:, t, c], start=(t == 0), stop=(t == TPB - 1))
                mm.then_inc(kv_ps, 1)

            def att(b):
                pe.wait_ge(kv_done, 4 * (b + 1))
                pe.wait_ge(qp_done, b + 1)
                for t in range(TPB):
                    for c in range(DC):
                        pe.matmul(PS[:, t, c * P:(c + 1) * P], qpT[:, c, t * P:(t + 1) * P], KV[:, c], start=True, stop=True)
                    for c in range(DC):
                        mm = pe.matmul(PS[:, 2, t * HEADS:(t + 1) * HEADS], qpT[:, c, t * P:(t + 1) * P], KS[:, c],
                                       start=(c == 0), stop=(c == DC - 1))
                    mm.then_inc(att_ps, 1)

            def t2(b):
                pe.wait_ge(xns[1], TPB * (b + 1))
                pe.wait_ge(xo_done, TPB * (b + 1))
                pe.wait_ge(xT_lo, TPB * (b + 3) if not isinstance(b, int) else TPB * min(b + 3, B))
                transpose_tiles(xn[1], 6, trs[1])

            def step(b, first=False, last=False):
                qproj(b)
                pe.wait_ge(w_lo, 2)
                pe.wait_ge(at_done, TPB * b)
                token_proj(1, xTh, xTl, 0, k_ps)
                if not first:
                    att_t(b - 1)
                pe.wait_ge(w_lo, 3)
                token_proj(2, xTh, xTl, 2, v_ps)
                if not first:
                    pe.wait_ge(wo_lo, 1)
                    oproj(b - 1)
                kv(b)
                if not last:
                    t1(b + 1)
                att(b)
                if not first:
                    t2(b - 1)

            pe.wait_ge(consts_in, 16 * 7)
            t1(0)
            pe.wait_ge(w_hi, 1)
            pe.wait_ge(w_lo, 1)
            step(0, first=True)
            step(1)
            with pe.Fori(2, B - 1) as b:
                step(b)
            step(B - 1, last=True)
            att_t(B - 1)
            oproj(B - 1)
            t2(B - 1)
        block1.__exit__(None, None, None)
        st1.close()
        ws = [sb(f"ws{w}", [P, DC + IC, D]) for w in range(2)]
        wh = [sb(f"wh{w}", [P, DC + IC, D], F32R) for w in range(2)]
        wl = [sb(f"wl{w}", [P, DC + IC, D], F32R) for w in range(2)]
        ws_in = [sem(f"ws_in{w}") for w in range(2)]
        gw = sb("gw", [P, DC, NE])
        gwh = sb("gwh", [P, DC, NE], F32R)
        gwl = sb("gwl", [P, DC, NE], F32R)
        zrow = sb("zrow", [P, D])
        gw_in, zero_done, zero_out = sem("gw_in"), sem("zero_done"), sem("zero_out")
        fixed_hi, fixed_lo = sem("fixed_hi"), sem("fixed_lo")

        def load_expert(sp, e, w):
            sp.dma_start(ws[w][:, 0:DC], gu_w[e]).then_inc(ws_in[w], 16)
            sp.dma_start(ws[w][:, DC:], dn_w[e]).then_inc(ws_in[w], 16)

        st2 = ExitStack()

        def sb2(name, shape, dt=F32):
            return st2.enter_context(nc.sbuf_tensor(name, shape, dt))
        LB = DC * B
        prod = [sb2(f"prod{k}", [P, DC, B, NPAIR]) for k in range(2)]
        Q2 = [sb2(f"Q2{k}", [P, LB, 2 * CD]) for k in range(2)]
        Y = [sb2(f"Y{k}", [P, LB, NPAIR]) for k in range(2)]
        term = [sb2(f"term{k}", [P, LB, CD, CD]) for k in range(2)]
        prod_done = [sem(f"prod_done{k}") for k in range(2)]
        conv_ps = [sem(f"conv_ps{k}") for k in range(2)]
        q2_done = [sem(f"q2_done{k}") for k in range(2)]
        y_done = [sem(f"y_done{k}") for k in range(2)]
        term_dve = [sem(f"term_dve{k}") for k in range(2)]
        term_pool = [sem(f"term_pool{k}") for k in range(2)]
        reduced = [sem(f"reduced{k}") for k in range(2)]
        NM = 7
        QYh = QY[:].rearrange("p c b s -> p (c b) s")

        with nc.Block() as block_:
            @block_.sync
            def _(sp):
                load_expert(sp, NE, 1)
                sp.dma_start(gw[:], gateT.rearrange("(c p) n -> p c n", p=P)).then_inc(gw_in, 16)
                sp.wait_ge(zero_done, 1)
                for t in range(SLOT_T):
                    rows = slice(B * S + t * P, B * S + (t + 1) * P)
                    sp.dma_start(xs_d[rows], zrow[:]).then_inc(zero_out, 16)
                    sp.dma_start(out[rows], zrow[:]).then_inc(zero_out, 16)
                with sp.Fori(0, CH // 2 - 1) as i:
                    for k in range(2):
                        sp.wait_ge(conv_ps[k], DC * (i + 1))
                        load_head(sp, 2 * i + 2 + k, k)
            @block_.gpsimd
            def _(pool):
                def products(i, k):
                    pool.wait_ge(tc_in[k], 32 * (i + 1))
                    pool.wait_ge(conv_ps[k], DC * i)
                    o = prod[k][:].rearrange("p c b n -> p (c b) n")
                    a = C2[k][:]
                    shifted = bass.AP(tensor=a.tensor, offset=a.offset, ap=[a.ap[0], a.ap[1], [1, 4], [1, CD]])
                    nc.gpsimd.tensor_tensor(o[:, :, 0:4 * CD].rearrange("p a (s j) -> p a s j", s=4),
                                            a[:, :, 0:CD].unsqueeze(2).broadcast_to([P, LB, 4, CD]), shifted,
                                            ALU.mult).then_inc(prod_done[k], 1)
                    nc.gpsimd.tensor_tensor(o[:, :, 4 * CD:], a[:, :, 0:4], a[:, :, 4:8], ALU.mult).then_inc(prod_done[k], 1)

                def half_term(i, k):
                    pool.wait_ge(y_done[k], DC * (i + 1))
                    pool.wait_ge(q2_done[k], i + 1)
                    pool.wait_ge(reduced[k], i)
                    nc.gpsimd.tensor_tensor(term[k][:, :, 7].rearrange("p a (t j) -> p a t j", t=2),
                                            Y[k][:, :, 4 * CD:].unsqueeze(2).broadcast_to([P, LB, 2, 4]),
                                            Q2[k][:, :, 4:12].rearrange("p a (t j) -> p a t j", t=2),
                                            ALU.mult).then_inc(term_pool[k], 1)

                nc.gpsimd.memset(zrow[:], 0.0).then_inc(zero_done, 1)
                def pair_of_heads(i):
                    products(i, 1)
                    half_term(i, 0)
                    products(i + 1, 0)
                    half_term(i, 1)

                products(0, 0)
                pair_of_heads(0)
                with pool.Fori(1, CH // 2 - 1) as i:
                    pair_of_heads(i)
                products(CH // 2 - 1, 1)
                half_term(CH // 2 - 1, 0)
                half_term(CH // 2 - 1, 1)

            @block_.scalar
            def _(act):
                act.wait_ge(gw_in, 16)
                act.activation(gwh[:], gw[:], ACT.Copy).then_inc(fixed_hi, 1)
                act.wait_ge(ws_in[1], 32)
                act.activation(wh[1][:], ws[1][:], ACT.Copy).then_inc(fixed_hi, 1)
                def pair_of_heads(i):
                    for k in range(2):
                        wait_apart(act, reduced[k], i)
                        act.activation(Q2[k][:].rearrange("p a (t j) -> p a t j", t=2),
                                       QYh[:, :, bass.ds((2 * i + k) * CD, CD)].unsqueeze(2).broadcast_to([P, LB, 2, CD]),
                                       ACT.Copy).then_inc(q2_done[k], 1)
                        for c in range(DC):
                            act.wait_ge(conv_ps[k], DC * i + c + 1)
                            act.activation(Y[k][:, c * B:(c + 1) * B].rearrange("p b n -> p (b n)"),
                                           PS[:, DC * k + c, 0:B * NPAIR], ACT.Copy).then_inc(y_done[k], 1)

                pair_of_heads(0)
                with act.Fori(1, CH // 2) as i:
                    pair_of_heads(i)

            @block_.vector
            def _(dve):
                def terms(i, k):
                    dve.wait_ge(y_done[k], DC * (i + 1))
                    dve.wait_ge(q2_done[k], i + 1)
                    y, q, t = Y[k][:], Q2[k][:], term[k]
                    shifted = bass.AP(tensor=q.tensor, offset=q.offset, ap=[q.ap[0], q.ap[1], [1, 4], [1, CD]])
                    dve.tensor_tensor(t[:, :, 0:4], y[:, :, 0:4 * CD].rearrange("p a (s j) -> p a s j", s=4),
                                      shifted, ALU.mult).then_inc(term_dve[k], 1)
                    for r in range(1, 4):
                        dve.tensor_tensor(t[:, :, 3 + r, r:CD], y[:, :, r * CD:(r + 1) * CD - r], q[:, :, 0:CD - r],
                                          ALU.mult).then_inc(term_dve[k], 1)
                        dve.tensor_tensor(t[:, :, 3 + r, 0:r], y[:, :, (r + 1) * CD - r:(r + 1) * CD], q[:, :, CD - r:CD],
                                          ALU.mult).then_inc(term_dve[k], 1)

                def reduce(i, k):
                    dve.wait_ge(term_dve[k], NM * (i + 1))
                    wait_apart(dve, term_pool[k], i + 1)
                    dve.tensor_reduce(QYh[:, :, bass.ds((2 * i + k) * CD, CD)],
                                      term[k][:].rearrange("p a s m -> p a m s"), AX_X, ALU.add).then_inc(reduced[k], 1)

                dve.wait_ge(fixed_hi, 1)
                dve.tensor_tensor(gwl[:], gw[:], gwh[:].bitcast(F32), ALU.subtract).then_inc(fixed_lo, 1)
                dve.wait_ge(fixed_hi, 2)
                dve.tensor_tensor(wl[1][:], ws[1][:], wh[1][:].bitcast(F32), ALU.subtract).then_inc(fixed_lo, 1)
                with dve.Fori(0, CH // 2) as i:
                    for k in range(2):
                        terms(i, k)
                        reduce(i, k)

            @block_.tensor
            def _(pe):
                def pair_of_heads(i):
                    for k in range(2):
                        pe.wait_ge(prod_done[k], 2 * (i + 1))
                        pe.wait_ge(y_done[k], DC * i)
                        for c in range(DC):
                            for m in range(c + 1):
                                mm = pe.matmul(PS[:, DC * k + c, 0:B * NPAIR], Tz[k][:, (c - m) * P:(c - m + 1) * P],
                                               prod[k][:, m].rearrange("p b n -> p (b n)"), start=(m == 0), stop=(m == c))
                            mm.then_inc(conv_ps[k], 1)

                pair_of_heads(0)
                with pe.Fori(1, CH // 2) as i:
                    pair_of_heads(i)
        st2.close()
        x3h = [sb(f"x3h{p}", [P, DC, P], F32R) for p in range(2)]
        x3l = [sb(f"x3l{p}", [P, DC, P], F32R) for p in range(2)]
        sg = [sb(f"sg{p}", [P, I_FF]) for p in range(2)]
        hh = [sb(f"hh{p}", [P, I_FF]) for p in range(2)]
        hTh = [sb(f"hTh{p}", [P, IC, P], F32R) for p in range(2)]
        hTl = [sb(f"hTl{p}", [P, IC, P], F32R) for p in range(2)]
        LG = sb("LG", [P, NT, NE])
        table_row = sb("table_row", [P, 1])
        st3 = ExitStack()

        def sb3(name, shape, dt=F32):
            return st3.enter_context(nc.sbuf_tensor(name, shape, dt))
        ysl = [sb3(f"ysl{p}", [P, DC, P]) for p in range(2)]
        xn3 = [sb3(f"xn3{p}", [P, D]) for p in range(2)]
        bst3 = [sb3(f"bn_stat3{p}", [P, 6]) for p in range(2)]
        mv3 = [sb3(f"mean_var3{p}", [P, 2]) for p in range(2)]
        ve3 = [sb3(f"var_eps3{p}", [P, 1]) for p in range(2)]
        rs3 = [sb3(f"rstd3{p}", [P, 1]) for p in range(2)]

        def pair(name):
            return [sem(f"{name}{p}") for p in range(2)]
        ysl_done, t3_ps, x2_done, bn3, mv3s, ve3s, rs3s, xn3_done = (
            pair(n) for n in ("ysl_done", "t3_ps", "x2_done", "ln2_bn", "ln2_mv", "ln2_ve", "ln2_rstd", "ln2_xn"))
        xs_out, t4_ps, x3_hi, x3_lo, rt_ps, lg_done, gu_ps, silu_done, h_done = (
            pair(n) for n in ("xs_out", "t4_ps", "x3_hi", "x3_lo", "rt_ps", "lg_done", "gu_ps", "silu_done", "h_done"))
        t5_ps, h_hi, h_lo, dn_ps, x3_done = (pair(n) for n in ("t5_ps", "h_hi", "h_lo", "dn_ps", "x3_done"))
        x3_out = sem("x3_out")

        def split_psum(act, dve, ps, n, hi, lo, ready, hi_done, lo_done, bank, width):
            if act is not None:
                act.wait_ge(ready, n + 1)
                act.activation(hi[:], bank, ACT.Copy).then_inc(hi_done, 1)
            else:
                dve.wait_ge(hi_done, n + 1)
                dve.tensor_tensor(lo[:], bank, hi[:].bitcast(F32), ALU.subtract).then_inc(lo_done, 1)

        def three_pass(pe, out_, lh, ll, rh, rl, first, last):
            pe.matmul(out_, lh, rh, start=first, stop=False)
            pe.matmul(out_, lh, rl, start=False, stop=False)
            return pe.matmul(out_, ll, rh, start=False, stop=last)

        def bank_chunks(bank, c=DC):
            return PS[:, bank, 0:c * P].rearrange("p (c n) -> p c n", c=c)

        def gate_up(pe, p, w, done):
            for c in range(DC):
                mm = three_pass(pe, PS[:, 3 + p], x3h[p][:, c], x3l[p][:, c], wh[w][:, c], wl[w][:, c], c == 0, c == DC - 1)
            mm.then_inc(done, 1)

        def down(pe, p, w, done):
            for c in range(IC):
                mm = three_pass(pe, PS[:, 6 + p], hTh[p][:, c], hTl[p][:, c], wh[w][:, DC + c], wl[w][:, DC + c],
                                c == 0, c == IC - 1)
            mm.then_inc(done, 1)

        with nc.Block() as block_:
            @block_.sync
            def _(sp):
                with sp.Fori(0, B) as i:
                    for p in range(2):
                        sp.wait_ge(xn3_done[p], i + 1)
                        sp.dma_start(xs_d[bass.ds((TPB * i + p) * P, P)], xn3[p][:]).then_inc(xs_out[p], 16)
                for p in range(2):
                    sp.wait_ge(x3_done[p], B)
                sp.dma_start(out[0:B * S].rearrange("(t p) n -> p t n", p=P), X[:]).then_inc(x3_out, 16)
                sp.wait_ge(x3_out, 16)
                sp.wait_ge(zero_out, 32 * SLOT_T)
                for p in range(2):
                    sp.wait_ge(xs_out[p], 16 * B)

            @block_.gpsimd
            def _(pool):
                def rstd3(i, p):
                    wait_apart(pool, mv3s[p], i + 1)
                    nc.gpsimd.tensor_scalar(ve3[p][:], mv3[p][:, 1:2], LN_EPS, None, ALU.add).then_inc(ve3s[p], 1)
                    pool.wait_ge(ve3s[p], i + 1)
                    nc.gpsimd.tensor_tensor(rs3[p][:], ve3[p][:], nhalf[:, 0:1], ALU.pow).then_inc(rs3s[p], 1)

                with pool.Fori(0, B) as i:
                    for p in range(2):
                        rstd3(i, p)

            @block_.scalar
            def _(act):
                def stage_y(i, p, first=False):
                    if not first:
                        wait_apart(act, t3_ps[p], i)
                    act.activation(ysl[p][:], QY[:, :, i, p * P:(p + 1) * P], ACT.Copy).then_inc(ysl_done[p], 1)

                def x_hi(i, p):
                    act.wait_ge(t4_ps[p], i + 1)
                    act.activation(x3h[p][:], bank_chunks(1), ACT.Copy).then_inc(x3_hi[p], 1)

                def silu(i, p):
                    act.wait_ge(gu_ps[p], i + 1)
                    act.activation(sg[p][:], PS[:, 3 + p, 0:I_FF], ACT.Silu).then_inc(silu_done[p], 1)

                def hid_hi(i, p):
                    act.wait_ge(t5_ps[p], i + 1)
                    act.activation(hTh[p][:], bank_chunks(5, IC), ACT.Copy).then_inc(h_hi[p], 1)

                def step(i, p, last=False):
                    if not last or p == 0:
                        x_hi(i + p, 1 - p)
                    silu(i, p)
                    if not last and not (p == 1 and isinstance(i, int) and i == B - 2):
                        stage_y(i + 1 + p, 1 - p)
                    hid_hi(i, p)

                act.activation(table_row[:], ident[:, 0:1], ACT.Silu)
                stage_y(0, 0, first=True)
                stage_y(0, 1, first=True)
                stage_y(1, 0)
                x_hi(0, 0)
                with act.Fori(0, B - 2) as i:
                    for p in range(2):
                        step(i, p)
                step(B - 2, 0)
                step(B - 2, 1)
                step(B - 1, 0, last=True)
                step(B - 1, 1, last=True)

            @block_.vector
            def _(dve):
                def x2(i, p):
                    dve.wait_ge(t3_ps[p], i + 1)
                    dve.tensor_tensor(X[:, TPB * i + p], X[:, TPB * i + p], PS[:, 0], ALU.add).then_inc(x2_done[p], 1)
                    wait_apart(dve, x2_done[p], i + 1)
                    dve.bn_stats(bst3[p][:], X[:, TPB * i + p]).then_inc(bn3[p], 1)
                    wait_apart(dve, bn3[p], i + 1)
                    dve.bn_aggr(mv3[p][:], bst3[p][:]).then_inc(mv3s[p], 1)

                def norm(i, p):
                    dve.wait_ge(xs_out[p], 16 * i)
                    dve.wait_ge(t4_ps[p], i)
                    dve.wait_ge(rs3s[p], i + 1)
                    dve.tensor_scalar(xn3[p][:], X[:, TPB * i + p], mv3[p][:, 0:1], rs3[p][:], ALU.subtract,
                                      ALU.mult).then_inc(xn3_done[p], 1)

                def x_lo(i, p):
                    dve.wait_ge(x3_hi[p], i + 1)
                    dve.tensor_tensor(x3l[p][:], bank_chunks(1), x3h[p][:].bitcast(F32), ALU.subtract).then_inc(x3_lo[p], 1)

                def hidden(i, p):
                    dve.wait_ge(silu_done[p], i + 1)
                    dve.tensor_tensor(hh[p][:], PS[:, 3 + p, I_FF:2 * I_FF], sg[p][:], ALU.mult).then_inc(h_done[p], 1)

                def logits(i, p):
                    wait_apart(dve, rt_ps[p], i + 1)
                    dve.tensor_copy(LG[:, TPB * i + p], PS[:, 2, 0:NE]).then_inc(lg_done[p], 1)

                def hid_lo(i, p):
                    dve.wait_ge(h_hi[p], i + 1)
                    dve.tensor_tensor(hTl[p][:], bank_chunks(5, IC), hTh[p][:].bitcast(F32), ALU.subtract).then_inc(h_lo[p], 1)

                def add_shared(i, p):
                    dve.wait_ge(dn_ps[p], i + 1)
                    dve.tensor_tensor(X[:, TPB * i + p], X[:, TPB * i + p], PS[:, 6 + p], ALU.add).then_inc(x3_done[p], 1)

                def step(i, p, first=False, last=False):
                    if not last or p == 0:
                        x_lo(i + p, 1 - p)
                    if not last:
                        x2(i + 1, p)
                    hidden(i, p)
                    if not last:
                        norm(i + 1, p)
                    logits(i, p)
                    if not first:
                        add_shared(i + p - 1, 1 - p)
                    hid_lo(i, p)

                x2(0, 0)
                norm(0, 0)
                x2(0, 1)
                x_lo(0, 0)
                norm(0, 1)
                step(0, 0, first=True)
                step(0, 1)
                step(1, 0)
                step(1, 1)
                with dve.Fori(2, B - 1) as i:
                    for p in range(2):
                        step(i, p)
                step(B - 1, 0, last=True)
                step(B - 1, 1, last=True)
                add_shared(B - 1, 1)

            @block_.tensor
            def _(pe):
                def t3(i, p, before):
                    pe.wait_ge(ysl_done[p], i + 1)
                    pe.wait_ge(x2_done[1 - p], before)
                    for c in range(DC):
                        mm = pe.transpose(PS[:, 0, c * P:(c + 1) * P], ysl[p][:, c], ident[:])
                    mm.then_inc(t3_ps[p], 1)

                def t4(i, p, before):
                    pe.wait_ge(xn3_done[p], i + 1)
                    pe.wait_ge(x3_lo[1 - p], before)
                    for c in range(DC):
                        mm = pe.transpose(PS[:, 1, c * P:(c + 1) * P], xn3[p][:, c * P:(c + 1) * P], ident[:])
                    mm.then_inc(t4_ps[p], 1)

                def router(i, p, before):
                    pe.wait_ge(lg_done[1 - p], before)
                    for c in range(DC):
                        mm = three_pass(pe, PS[:, 2, 0:NE], x3h[p][:, c], x3l[p][:, c], gwh[:, c], gwl[:, c], c == 0, c == DC - 1)
                    mm.then_inc(rt_ps[p], 1)

                def t5(i, p, before):
                    pe.wait_ge(h_done[p], i + 1)
                    pe.wait_ge(h_lo[1 - p], before)
                    for c in range(IC):
                        mm = pe.transpose(PS[:, 5, c * P:(c + 1) * P], hh[p][:, c * P:(c + 1) * P], ident[:])
                    mm.then_inc(t5_ps[p], 1)

                def step(i, p, first=False, last=False):
                    if not last or p == 0:
                        t4(i + p, 1 - p, i + 1)
                    if not last:
                        t3(i + 1, p, i + p + 1)
                    pe.wait_ge(x3_lo[p], i + 1)
                    pe.wait_ge(h_done[p], i)
                    gate_up(pe, p, 1, gu_ps[p])
                    router(i, p, i + p)
                    if not first:
                        pe.wait_ge(h_lo[1 - p], i + p)
                        pe.wait_ge(x3_done[1 - p], i + p - 1)
                        down(pe, 1 - p, 1, dn_ps[1 - p])
                    t5(i, p, i + p)

                t3(0, 0, 0)
                t3(0, 1, 1)
                t4(0, 0, 0)
                step(0, 0, first=True)
                step(0, 1)
                step(1, 0)
                step(1, 1)
                with pe.Fori(2, B - 1) as i:
                    for p in range(2):
                        step(i, p)
                step(B - 1, 0, last=True)
                step(B - 1, 1, last=True)
                pe.wait_ge(h_lo[1], B)
                pe.wait_ge(x3_done[1], B - 1)
                down(pe, 1, 1, dn_ps[1])
        st3.close()
        W4 = sb("W4", [P, NT, TOPK])
        IDX = sb("IDX", [P, NCOL], U32)
        WPOS = sb("WPOS", [P, NCOL])
        ES = sb("ES", [P, NSLOT], I32)
        MORE = sb("MORE", [P, 1], I32)
        st4 = ExitStack()

        def sb4(name, shape, dt=F32):
            return st4.enter_context(nc.sbuf_tensor(name, shape, dt))
        eb = sb4("eb", [P, NE])
        lt4 = sb4("lt4", [P, 4, 4])
        tri = sb4("tri", [P, P])
        free = sb4("free", [P, P])
        slotk = sb4("slotk", [P, B * S // SLOT])
        tok = sb4("tok", [P, NT + SLOT_T])
        ones = sb4("ones", [P, P])
        SC = sb4("SC", [P, NT, NE])
        BI = sb4("BI", [P, NT, NE])
        MB = sb4("MB", [P, NT, NE])
        g_hi, g_lo = sb4("g_hi", [P, NT * 4, 2]), sb4("g_lo", [P, NT * 4, 2])
        g_a, g_b, g_c, GS = (sb4(n, [P, NT * 4]) for n in ("g_a", "g_b", "g_c", "GS"))
        g_gt, g_eq = sb4("g_gt", [P, NT, 4, 4]), sb4("g_eq", [P, NT, 4, 4])
        V8 = sb4("V8", [P, NT, 8])
        I8 = sb4("I8", [P, NT, 8], U32)
        EF = sb4("EF", [P, NT, TOPK])
        OH = sb4("OH", [P, NT, TOPK, NE])
        OT = sb4("OT", [P, NT, TOPK, NE])
        WS = sb4("WS", [P, NT, TOPK])
        dsum, drec = sb4("dsum", [P, NT]), sb4("drec", [P, NT])
        SEL = sb4("SEL", [P, NT, NE])
        TOT = sb4("TOT", [P, NT, NE])
        acc = [sb4(f"acc{i}", [P, NT, NE]) for i in range(2)]
        NSK = sb4("NSK", [P, NE, B * S // SLOT])
        NS = sb4("NS", [P, NE])
        se = [sb4(f"se{i}", [P, NE]) for i in range(2)]
        base = sb4("base", [P, NE])
        POS = sb4("POS", [P, NT, NE])
        DEST = sb4("DEST", [P, NT, TOPK])
        DI, LOWI, HII = (sb4(n, [P, NT, TOPK], I32) for n in ("DI", "LOWI", "HII"))
        LOW, HIF, TOKV = (sb4(n, [P, NT, TOPK]) for n in ("LOW", "HIF", "TOKV"))
        LAST = sb4("LAST", [P, 1], I32)
        SLE = sb4("SLE", [P, NSLOT, NE])
        ESF = sb4("ESF", [P, NSLOT])
        lowhot = [sb4(f"lowhot{r}", [P, P]) for r in range(TOPK)]
        colhot = [sb4(f"colhot{r}", [P, 2, NCOL]) for r in range(TOPK)]
        r_in, r_one, score_done, chain = sem("r_in"), sem("r_one"), sem("score_done"), sem("route_step")
        sel_done, count_ps = sem("sel_done"), sem("count_ps")
        hot_done = sem("hot_done")
        hot_used = [sem(f"hot_used{r}") for r in range(TOPK)]

        with nc.Block() as block_:
            @block_.sync
            def _(sp):
                sp.dma_start(eb[:], bass.AP(tensor=ebias.tensor, offset=0, ap=[[0, P], [1, NE]])).then_inc(r_in, 16)
                for dst, src in ((lt4, c_lt4), (tri, c_tri), (free, c_free), (slotk, c_slotk), (tok, c_tok)):
                    sp.dma_start(dst[:], src).then_inc(r_in, 16)

            @block_.scalar
            def _(act):
                act.activation(SC[:], LG[:], ACT.Sigmoid).then_inc(score_done, 1)

            @block_.tensor
            def _(pe):
                pe.wait_ge(sel_done, 1)
                pe.wait_ge(r_in, 16 * 6)
                pe.wait_ge(r_one, 1)
                sel = SEL[:].rearrange("p t e -> p (t e)")
                pe.matmul(PS[:, 0, 0:NT * NE], tri[:], sel, start=True, stop=True)
                pe.matmul(PS[:, 1, 0:NT * NE], ones[:], sel, start=True, stop=True).then_inc(count_ps, 1)

                def place(t, first=False, last=False):
                    for r in range(TOPK):
                        pe.wait_ge(hot_done, 3 * (TOPK * t + r + 1))
                        mm = pe.matmul(PS[:, 2, 0:2 * NCOL], lowhot[r][:], colhot[r][:].rearrange("p a c -> p (a c)"),
                                       start=(first and r == 0), stop=(last and r == TOPK - 1))
                        mm.then_inc(hot_used[r], 1)
                place(0, first=True)
                with pe.Fori(1, NT - 1) as t:
                    place(t)
                place(NT - 1, last=True)

            @block_.gpsimd
            def _(pool):
                nc.gpsimd.memset(ones[:], 1.0).then_inc(r_one, 1)

            @block_.vector
            def _(dve):
                steps = [0]

                def link(ins):
                    steps[0] += 1
                    ins.then_inc(chain, 1)
                    dve.wait_ge(chain, steps[0])

                def tt(o, a, b, op):
                    link(dve.tensor_tensor(o, a, b, op))

                def reduce(o, a):
                    link(dve.tensor_reduce(o, a, AX_X, ALU.add))

                dve.wait_ge(r_in, 16 * 6)
                dve.wait_ge(score_done, 1)
                tt(BI[:], SC[:], eb[:].unsqueeze(1).broadcast_to([P, NT, NE]), ALU.add)
                quad = BI[:].rearrange("p t (g k) -> p (t g) k", k=4)
                tt(g_hi[:], quad[:, :, 0:4:2], quad[:, :, 1:4:2], ALU.max)
                tt(g_lo[:], quad[:, :, 0:4:2], quad[:, :, 1:4:2], ALU.min)
                tt(g_a[:], g_hi[:, :, 0], g_hi[:, :, 1], ALU.max)
                tt(g_b[:], g_hi[:, :, 0], g_hi[:, :, 1], ALU.min)
                tt(g_c[:], g_lo[:, :, 0], g_lo[:, :, 1], ALU.max)
                tt(g_b[:], g_b[:], g_c[:], ALU.max)
                tt(GS[:], g_a[:], g_b[:], ALU.add)
                gs = GS[:].rearrange("p (t g) -> p t g", g=4)
                other = gs.unsqueeze(2).broadcast_to([P, NT, 4, 4])
                own = gs.unsqueeze(3).broadcast_to([P, NT, 4, 4])
                tt(g_gt[:], other, own, ALU.is_gt)
                tt(g_eq[:], other, own, ALU.is_equal)
                tt(g_eq[:].rearrange("p t g h -> p t (g h)"), g_eq[:].rearrange("p t g h -> p t (g h)"),
                   lt4[:].rearrange("p g h -> p (g h)").unsqueeze(1).broadcast_to([P, NT, 16]), ALU.mult)
                tt(g_gt[:], g_gt[:], g_eq[:], ALU.add)
                reduce(g_a[:], g_gt[:].rearrange("p t g h -> p (t g) h"))
                link(dve.tensor_scalar(g_b[:], g_a[:], 1.5, None, ALU.is_lt))
                link(dve.tensor_scalar(g_c[:], g_b[:], BIG, -BIG, ALU.mult, ALU.add))
                mquad = MB[:].rearrange("p t (g k) -> p (t g) k", k=4)
                tt(mquad, quad, g_b[:].unsqueeze(2).broadcast_to([P, NT * 4, 4]), ALU.mult)
                tt(mquad, mquad, g_c[:].unsqueeze(2).broadcast_to([P, NT * 4, 4]), ALU.add)
                for t in range(NT):
                    steps[0] += 1
                    dve.max(V8[:, t], MB[:, t]).then_inc(chain, 1)
                dve.wait_ge(chain, steps[0])
                for t in range(NT):
                    steps[0] += 1
                    dve.max_index(I8[:, t], V8[:, t], MB[:, t]).then_inc(chain, 1)
                dve.wait_ge(chain, steps[0])
                link(dve.tensor_copy(EF[:], I8[:, :, 0:TOPK]))
                oh = OH[:].rearrange("p t r e -> p (t r) e")
                tt(oh, EF[:].rearrange("p t r -> p (t r)").unsqueeze(2).broadcast_to([P, NT * TOPK, NE]),
                   free[:, 0:NE].unsqueeze(1).broadcast_to([P, NT * TOPK, NE]), ALU.is_equal)
                dve.tensor_reduce(SEL[:], OH[:].rearrange("p t r e -> p t e r"), AX_X, ALU.add).then_inc(sel_done, 1)
                tt(OT[:], OH[:], SC[:].unsqueeze(2).broadcast_to([P, NT, TOPK, NE]), ALU.mult)
                reduce(WS[:], OT[:])
                reduce(dsum[:], WS[:])
                link(dve.tensor_scalar(dsum[:], dsum[:], 1e-20, None, ALU.add))
                link(dve.reciprocal(drec[:], dsum[:]))
                tt(W4[:], WS[:], drec[:].unsqueeze(2).broadcast_to([P, NT, TOPK]), ALU.mult)
                link(dve.tensor_scalar(W4[:], W4[:], 2.5, None, ALU.mult))
                dve.wait_ge(count_ps, 1)
                link(dve.tensor_copy(TOT[:].rearrange("p t e -> p (t e)"), PS[:, 1, 0:NT * NE]))
                cur, k, n = TOT, 1, 0
                while k < NT:
                    nxt = acc[n % 2]
                    link(dve.tensor_copy(nxt[:, 0:k], cur[:, 0:k]))
                    tt(nxt[:, k:], cur[:, k:], cur[:, 0:NT - k], ALU.add)
                    cur, k, n = nxt, 2 * k, n + 1
                tt(NSK[:], cur[:, NT - 1].unsqueeze(2).broadcast_to([P, NE, B * S // SLOT]),
                   slotk[:].unsqueeze(1).broadcast_to([P, NE, B * S // SLOT]), ALU.is_gt)
                reduce(NS[:], NSK[:])
                tt(POS[:], cur[:], TOT[:], ALU.subtract)
                cur, k, n = NS, 1, 0
                while k < NE:
                    nxt = se[n % 2]
                    link(dve.tensor_copy(nxt[:, 0:k], cur[:, 0:k]))
                    tt(nxt[:, k:], cur[:, k:], cur[:, 0:NE - k], ALU.add)
                    cur, k, n = nxt, 2 * k, n + 1
                ends = cur
                tt(base[:], ends[:], NS[:], ALU.subtract)
                link(dve.tensor_scalar(base[:], base[:], float(SLOT), None, ALU.mult))
                tt(SLE[:], ends[:].unsqueeze(1).broadcast_to([P, NSLOT, NE]),
                   free[:, 0:NSLOT].unsqueeze(2).broadcast_to([P, NSLOT, NE]), ALU.is_le)
                reduce(ESF[:], SLE[:])
                link(dve.tensor_scalar(ES[:], ESF[:], float(NE - 1), None, ALU.min))
                link(dve.tensor_scalar(LAST[:], ends[:, NE - 1:NE], -1.0, None, ALU.add))
                link(dve.tensor_scalar(LAST[:], LAST[:], 1, None, ALU.arith_shift_right))
                link(dve.tensor_scalar(MORE[:], LAST[:], -float(NFULL - 1), None, ALU.add))
                tt(POS[:], POS[:], base[:].unsqueeze(1).broadcast_to([P, NT, NE]), ALU.add)
                tt(POS[:].rearrange("p t e -> p (t e)"), POS[:].rearrange("p t e -> p (t e)"), PS[:, 0, 0:NT * NE], ALU.add)
                tt(OT[:], OH[:], POS[:].unsqueeze(2).broadcast_to([P, NT, TOPK, NE]), ALU.mult)
                reduce(DEST[:], OT[:])
                link(dve.tensor_copy(DI[:], DEST[:]))
                link(dve.tensor_scalar(LOWI[:], DI[:], SLOT - 1, None, ALU.bitwise_and))
                link(dve.tensor_copy(LOW[:], LOWI[:]))
                tt(TOKV[:], tok[:, 0:NT].unsqueeze(2).broadcast_to([P, NT, TOPK]), LOW[:], ALU.subtract)
                link(dve.tensor_scalar(LOWI[:], DI[:], P - 1, None, ALU.bitwise_and))
                link(dve.tensor_scalar(HII[:], DI[:], 7, None, ALU.arith_shift_right))
                link(dve.tensor_copy(LOW[:], LOWI[:]))
                link(dve.tensor_copy(HIF[:], HII[:]))
                def one_hots(t):
                    for r in range(TOPK):
                        dve.wait_ge(hot_used[r], t)
                        dve.tensor_scalar(lowhot[r][:], free[:], LOW[:, t, r:r + 1], None, ALU.is_equal).then_inc(hot_done, 1)
                        dve.tensor_scalar(colhot[r][:, 0], free[:, 0:NCOL], HIF[:, t, r:r + 1], TOKV[:, t, r:r + 1],
                                          ALU.is_equal, ALU.mult).then_inc(hot_done, 1)
                        dve.tensor_scalar(colhot[r][:, 1], free[:, 0:NCOL], HIF[:, t, r:r + 1], W4[:, t, r:r + 1],
                                          ALU.is_equal, ALU.mult).then_inc(hot_done, 1)

                one_hots(0)
                with dve.Fori(1, NT) as t:
                    one_hots(t)
                dve.wait_ge(hot_used[TOPK - 1], NT)
                tt(IDX[:].rearrange("p (s t) -> p s t", t=SLOT_T), PS[:, 2, 0:NCOL].rearrange("p (s t) -> p s t", t=SLOT_T),
                   tok[:, NT:].unsqueeze(1).broadcast_to([P, NSLOT, SLOT_T]), ALU.add)
                link(dve.tensor_copy(WPOS[:], PS[:, 2, NCOL:2 * NCOL]))
        st4.close()

        RING = 2 * SLOT_T
        NIT = NSLOT // 2
        def last_pair(eng):
            return eng.value_load(MORE[0:1, 0:1], min_val=0, max_val=NIT - NFULL) + (NFULL - 1)

        def pairs_of_slots(eng, first, last, body):
            with eng.Fori(first, NFULL - 1) as i:
                body(i)
            with eng.Fori(NFULL - 1, NIT - 1) as i:
                with eng.If(i < last):
                    body(i)
        idx = [sb(f"idx{q}", [P, 1], U32) for q in range(RING)]
        idy = [sb(f"idy{q}", [P, 1], U32) for q in range(RING)]
        xg = [sb(f"xg{q}", [P, D]) for q in range(RING)]
        yo = [sb(f"yo{q}", [P, D]) for q in range(RING)]

        def ring(name):
            return [sem(f"{name}{q}") for q in range(RING)]
        xg_in = ring("xg_in")
        idx_done, idy_done = sem("idx_done"), sem("idy_done")
        yo_done = sem("yo_done")

        def count(i, q):
            return B + 2 * i + q // 2

        add_out = [sem(f"add_out{half}") for half in range(2)]
        w5_hi, w5_lo, w5_lop, ws5_in = pair("w5_hi"), pair("w5_lo"), pair("w5_lop"), pair("ws5_in")
        HALVES = ((0, 3), (3, DC + IC))

        def next_slot(i, q):
            return i + (q + 2) // RING, (q // 2 + 1) % 2

        with nc.Block() as block_:
            @block_.sync
            def _(sp):
                def load(slot, w):
                    e = sp.value_load(ES[0:1, bass.ds(slot, 1)], min_val=0, max_val=NE - 1)
                    sp.dma_start(ws[w][:, 0:DC], gu_w[bass.ds(e, 1)].rearrange("o p c n -> p (o c) n")).then_inc(ws5_in[w], 16)
                    sp.dma_start(ws[w][:, DC:], dn_w[bass.ds(e, 1)].rearrange("o p c n -> p (o c) n")).then_inc(ws5_in[w], 16)

                load(0, 0)
                load(1, 1)

                def next_pair(i):
                    for w in range(2):
                        wait_apart(sp, w5_hi[w], 2 * (i + 1))
                        wait_apart(sp, w5_lo[w], 2 * (i + 1))
                        wait_apart(sp, w5_lop[w], 2 * (i + 1))
                        load(2 * i + 2 + w, w)

                pairs_of_slots(sp, 0, last_pair(sp), next_pair)

            @block_.gpsimd
            def _(pool):
                def ahead(i, q, n):
                    return i + (q + n) // RING, (q + n) % RING

                def gather(i, q):
                    nc.gpsimd.tensor_copy(idx[q][:], IDX[:, bass.ds(RING * i + q, 1)]).then_inc(idx_done, 1)
                    wait_apart(pool, idx_done, RING * i + q + 1)
                    nc.gpsimd.indirect_dma_start(out=xg[q][:], out_offset=None, in_=xs_d,
                                                 in_offset=bass.IndirectOffsetOnAxis(ap=idx[q][:, 0:1], axis=0)
                                                 ).then_inc(xg_in[q], 16)

                def scatter(i, q):
                    nc.gpsimd.tensor_copy(idy[q][:], IDX[:, bass.ds(RING * i + q, 1)]).then_inc(idy_done, 1)
                    wait_apart(pool, idy_done, RING * i + q + 1)
                    wait_apart(pool, yo_done, RING * i + q + 1)
                    if q % 2 == 0:
                        for half in range(2):
                            wait_apart(pool, add_out[half], 16 * (2 * i + q // 2))
                    nc.gpsimd.indirect_dma_start(out=out, out_offset=bass.IndirectOffsetOnAxis(ap=idy[q][:, 0:1], axis=0),
                                                 in_=yo[q][:], in_offset=None, compute_op=ALU.add
                                                 ).then_inc(add_out[q % 2], 16)

                def w_lo_pool(i, w, half):
                    c = HALVES[half][1] - 1
                    pool.wait_ge(w5_hi[w], 2 * i + half + 1)
                    nc.gpsimd.tensor_tensor(wl[w][:, c], ws[w][:, c], wh[w][:, c].bitcast(F32), ALU.subtract
                                            ).then_inc(w5_lop[w], 1)

                def step(i, q, first=False, last=False):
                    if not (last and q >= 1):
                        i3, q3 = ahead(i, q, 3)
                        wait_apart(pool, t4_ps[q3 % 2], count(i3, q3) - 1)
                        gather(i3, q3)
                    if not (last and q >= 2):
                        w_lo_pool(*next_slot(i, q), q % 2)
                    if q % 2 == 0 and not (first and q == 0):
                        for before in (2, 1):
                            scatter(i if q >= 2 else i - 1, (q - before) % RING)

                for q in range(3):
                    gather(0, q)
                w_lo_pool(0, 0, 0)
                w_lo_pool(0, 0, 1)
                for q in range(RING):
                    step(0, q, first=True)

                def four_tiles(i):
                    for q in range(RING):
                        step(i, q)

                last_i = last_pair(pool)
                pairs_of_slots(pool, 1, last_i, four_tiles)
                for q in range(RING):
                    step(last_i, q, last=True)
                scatter(last_i, 2)
                scatter(last_i, 3)
                for half in range(2):
                    wait_apart(pool, add_out[half], 16 * 2 * (last_i + 1))

            @block_.scalar
            def _(act):
                def x_hi(i, q):
                    p, n = q % 2, count(i, q)
                    act.wait_ge(t4_ps[p], n + 1)
                    act.activation(x3h[p][:], bank_chunks(p), ACT.Copy).then_inc(x3_hi[p], 1)

                def silu(i, q):
                    p, n = q % 2, count(i, q)
                    act.wait_ge(gu_ps[p], n + 1)
                    act.activation(sg[p][:], PS[:, 3 + p, 0:I_FF], ACT.Silu).then_inc(silu_done[p], 1)

                def hid_hi(i, q):
                    p, n = q % 2, count(i, q)
                    act.wait_ge(t5_ps[p], n + 1)
                    act.activation(hTh[p][:], bank_chunks(5, IC), ACT.Copy).then_inc(h_hi[p], 1)

                def w_hi_part(i, w, half):
                    a, b = HALVES[half]
                    act.wait_ge(ws5_in[w], 32 * (i + 1))
                    act.activation(wh[w][:, a:b], ws[w][:, a:b], ACT.Copy).then_inc(w5_hi[w], 1)

                def step(i, q, last=False):
                    if not (last and q == RING - 1):
                        x_hi(i + (q + 1) // RING, (q + 1) % RING)
                    if not (last and q >= 2):
                        w_hi_part(*next_slot(i, q), q % 2)
                    silu(i, q)
                    hid_hi(i, q)

                act.activation(table_row[:], ident[:, 0:1], ACT.Silu)
                w_hi_part(0, 0, 0)
                w_hi_part(0, 0, 1)
                x_hi(0, 0)

                def four_tiles(i):
                    for q in range(RING):
                        step(i, q)

                last_i = last_pair(act)
                pairs_of_slots(act, 0, last_i, four_tiles)
                for q in range(RING):
                    step(last_i, q, last=True)

            @block_.vector
            def _(dve):
                def x_lo(i, q):
                    p, n = q % 2, count(i, q)
                    dve.wait_ge(x3_hi[p], n + 1)
                    dve.tensor_tensor(x3l[p][:], bank_chunks(p), x3h[p][:].bitcast(F32), ALU.subtract).then_inc(x3_lo[p], 1)

                def hidden(i, q):
                    p, n = q % 2, count(i, q)
                    dve.wait_ge(silu_done[p], n + 1)
                    dve.scalar_tensor_tensor(out=hh[p][:], in0=PS[:, 3 + p, I_FF:2 * I_FF],
                                             scalar=WPOS[:, bass.ds(RING * i + q, 1)], in1=sg[p][:],
                                             op0=ALU.mult, op1=ALU.mult).then_inc(h_done[p], 1)

                def hid_lo(i, q):
                    p, n = q % 2, count(i, q)
                    dve.wait_ge(h_hi[p], n + 1)
                    dve.tensor_tensor(hTl[p][:], bank_chunks(5, IC), hTh[p][:].bitcast(F32), ALU.subtract).then_inc(h_lo[p], 1)

                def y_out(i, q):
                    p, n = q % 2, count(i, q)
                    if not (isinstance(i, int) and i == 0):
                        dve.wait_ge(add_out[p], 16 * (2 * i + q // 2 - 1))
                    dve.wait_ge(dn_ps[p], n + 1)
                    dve.tensor_copy(yo[q][:], PS[:, 6 + p]).then_inc(yo_done, 1)

                def w_lo_part(i, w, half):
                    a, b = HALVES[half]
                    dve.wait_ge(w5_hi[w], 2 * i + half + 1)
                    dve.tensor_tensor(wl[w][:, a:b - 1], ws[w][:, a:b - 1], wh[w][:, a:b - 1].bitcast(F32), ALU.subtract
                                      ).then_inc(w5_lo[w], 1)

                def step(i, q, first=False, last=False):
                    if not (last and q == RING - 1):
                        x_lo(i + (q + 1) // RING, (q + 1) % RING)
                    if not (last and q >= 2):
                        w_lo_part(*next_slot(i, q), q % 2)
                    hidden(i, q)
                    if not (first and q == 0):
                        y_out(*((i, q - 1) if q else (i - 1, RING - 1)))
                    hid_lo(i, q)

                w_lo_part(0, 0, 0)
                w_lo_part(0, 0, 1)
                x_lo(0, 0)
                for q in range(RING):
                    step(0, q, first=True)

                def four_tiles(i):
                    for q in range(RING):
                        step(i, q)

                last_i = last_pair(dve)
                pairs_of_slots(dve, 1, last_i, four_tiles)
                for q in range(RING):
                    step(last_i, q, last=True)
                y_out(last_i, RING - 1)

            @block_.tensor
            def _(pe):
                def t6(i, q):
                    p, n = q % 2, count(i, q)
                    pe.wait_ge(xg_in[q], 16 * (i + 1))
                    pe.wait_ge(x3_lo[p], n)
                    for c in range(DC):
                        mm = pe.transpose(PS[:, p, c * P:(c + 1) * P], xg[q][:, c * P:(c + 1) * P], ident[:])
                    mm.then_inc(t4_ps[p], 1)

                def t7(i, q):
                    p, n = q % 2, count(i, q)
                    pe.wait_ge(h_done[p], n + 1)
                    pe.wait_ge(h_lo[1 - p], n + p)
                    for c in range(IC):
                        mm = pe.transpose(PS[:, 5, c * P:(c + 1) * P], hh[p][:, c * P:(c + 1) * P], ident[:])
                    mm.then_inc(t5_ps[p], 1)

                def down5(i, q):
                    p, n, w = q % 2, count(i, q), q // 2
                    pe.wait_ge(h_lo[p], n + 1)
                    if not (isinstance(i, int) and RING * i + q < 2):
                        pe.wait_ge(yo_done, RING * i + q - 1)
                    down(pe, p, w, dn_ps[p])

                def gu5(i, q):
                    p, n, w = q % 2, count(i, q), q // 2
                    if p == 0:
                        pe.wait_ge(w5_lo[w], 2 * (i + 1))
                        pe.wait_ge(w5_lop[w], 2 * (i + 1))
                    pe.wait_ge(x3_lo[p], n + 1)
                    pe.wait_ge(h_done[p], n)
                    gate_up(pe, p, w, gu_ps[p])

                def step(i, q, first=False, last=False):
                    if not (last and q == RING - 1):
                        t6(i + (q + 1) // RING, (q + 1) % RING)
                    gu5(i, q)
                    if not (first and q == 0):
                        down5(*((i, q - 1) if q else (i - 1, RING - 1)))
                    t7(i, q)

                t6(0, 0)
                for q in range(RING):
                    step(0, q, first=True)

                def four_tiles(i):
                    for q in range(RING):
                        step(i, q)

                last_i = last_pair(pe)
                pairs_of_slots(pe, 1, last_i, four_tiles)
                for q in range(RING):
                    step(last_i, q, last=True)
                down5(last_i, RING - 1)


_NAMES = ["x", "ctx2", "qwT", "kwT", "vwT", "owT", "q_b", "k_b", "v_b", "o_b", "ssm", "dskip", "gateT", "ebias",
          "gu_w", "dn_w", "c_ident", "c_block", "c_head", "c_lt4", "c_tri", "c_free", "c_slotk",
          "c_tok"]


def lay_out(x, ctx_2048, L0_attn_q_w, L0_attn_q_b, L0_attn_k_w, L0_attn_k_b, L0_attn_v_w, L0_attn_v_b,
            L0_attn_o_w, L0_attn_o_b, L0_xattn_ssm_kernel, L0_xattn_D, L0_ffn_gate_weight, L0_ffn_expert_bias,
            L0_ffn_gate_proj, L0_ffn_up_proj, L0_ffn_down_proj, L0_ffn_shared_gate, L0_ffn_shared_up,
            L0_ffn_shared_down):
    f = np.ascontiguousarray
    c = np.asarray(ctx_2048).reshape(B, CH, CD, DC, P)[..., ::-1].transpose(1, 4, 3, 0, 2)
    c = np.concatenate([c, c], axis=-1)
    g = np.concatenate([np.asarray(L0_ffn_gate_proj), np.asarray(L0_ffn_shared_gate)[None]])
    u = np.concatenate([np.asarray(L0_ffn_up_proj), np.asarray(L0_ffn_shared_up)[None]])
    d = np.concatenate([np.asarray(L0_ffn_down_proj), np.asarray(L0_ffn_shared_down)[None]])
    gu = np.concatenate([g, u], axis=1).transpose(0, 2, 1).reshape(NE + 1, DC, P, 2 * I_FF).transpose(0, 2, 1, 3)
    dn = d.transpose(0, 2, 1).reshape(NE + 1, IC, P, D).transpose(0, 2, 1, 3)
    p = np.arange(P)
    e = np.arange(NE)
    vals = [
        f(x), f(c), f(np.asarray(L0_attn_q_w).T), f(np.asarray(L0_attn_k_w).T), f(np.asarray(L0_attn_v_w).T),
        f(np.asarray(L0_attn_o_w).T), f(np.asarray(L0_attn_q_b).reshape(DC, P).T), f(L0_attn_k_b), f(L0_attn_v_b), f(L0_attn_o_b),
        f(L0_xattn_ssm_kernel), f(np.asarray(L0_xattn_D)[:, None]), f(np.asarray(L0_ffn_gate_weight).T),
        f(L0_ffn_expert_bias), f(gu), f(dn),
        np.eye(P, dtype=np.float32),
        (p[:, None] // HD == p[None, :] // HD).astype(np.float32),
        ((np.arange(DC)[:, None] * GPD + p[:, None, None] // HD) == np.arange(HEADS)).astype(np.float32),
        np.broadcast_to((np.arange(4)[None, :] < np.arange(4)[:, None]).astype(np.float32), (P, 4, 4)).copy(),
        (p[:, None] < p[None, :]).astype(np.float32),
        np.broadcast_to(p.astype(np.float32), (P, P)).copy(),
        np.broadcast_to(np.arange(B * S // SLOT, dtype=np.float32) * SLOT, (P, B * S // SLOT)).copy(),
        np.concatenate([np.arange(NT)[None, :] * P + p[:, None] - B * S,
                        B * S + np.arange(SLOT_T)[None, :] * P + p[:, None]], axis=1).astype(np.float32),
    ]
    return dict(zip(_NAMES, vals))


def kernel(**inputs):
    import concourse.bacc as _bacc
    from concourse import mybir as _mybir
    from concourse.bass_utils import run_bass_kernel_spmd as _run

    nc = _bacc.Bacc("TRN2", target_bir_lowering=False, num_devices=1)
    arrays, args = {}, []
    for name, a in lay_out(**inputs).items():
        arrays[f"in_{name}"] = a
        args.append(nc.dram_tensor(f"in_{name}", a.shape, _mybir.dt.from_np(a.dtype), kind="ExternalInput").ap())
    out = nc.dram_tensor("out_y", (B * S + SLOT, D), F32, kind="ExternalOutput").ap()
    decoder_program(nc, *args, out)
    r = _run(nc, [arrays], core_ids=[0])
    return r.results[0]["out_y"][:B * S].reshape(B, S, D)
```

```python
from contextlib import ExitStack

import numpy as np

import concourse.bass as bass
from concourse import mybir

F32 = mybir.dt.float32
F32R = mybir.dt.float32r
I32 = mybir.dt.int32
U32 = mybir.dt.uint32
ALU = mybir.AluOpType
ACT = mybir.ActivationFunctionType
AX_X = mybir.AxisListType.X

P = 128
B, S, D = 8, 256, 512
NT = B * S // P
TPB = S // P
DC = D // P
HEADS, HD = 16, 32
CH, CD = 32, 8
NPAIR = CD * (CD + 1) // 2
GPD = P // HD
NE, I_FF = 16, 256
IC = I_FF // P
TOPK = 4
SLOT_T = 2
SLOT = SLOT_T * P
NSLOT = B * S * TOPK // SLOT + NE - 1
NSLOT += NSLOT % 2
NFULL = B * S * TOPK // SLOT // 2
NROW = NSLOT * SLOT
NCOL = NROW // P
LN_EPS = 1e-5
ATT_EPS = 1e-6
BIG = 3.0e38
KPAD = P - 1 + D


def decoder_program(nc, x, ctx2, qwT, kwT, vwT, owT, q_b, k_b, v_b, o_b, ssm, dskip, gateT, ebias,
                    gu_w, dn_w, c_ident, c_block, c_head, c_lt4, c_tri, c_free, c_slotk,
                    c_tok, out):
    with ExitStack() as ctx:
        def sb(name, shape, dt=F32):
            return ctx.enter_context(nc.sbuf_tensor(name, shape, dt))

        def sem(name):
            return ctx.enter_context(nc.semaphore(name))

        kpad_d = nc.dram_tensor("kpad_d", (CH, KPAD + 1), F32).ap()
        xs_d = nc.dram_tensor("xs_d", (B * S + SLOT, D), F32).ap()

        PS = ctx.enter_context(nc.psum_tensor("PS", [P, 8, 512], F32))

        X = sb("X", [P, NT, D])
        ident = sb("ident", [P, P])
        nhalf = sb("nhalf", [P, TPB])
        Tz = [sb(f"Tz{k}", [P, D]) for k in range(2)]
        C2 = [sb(f"C2{k}", [P, DC * B, 2 * CD]) for k in range(2)]
        LB = DC * B
        prod = [sb("prod0", [P, DC, B, NPAIR])]
        prod_done = [sem(f"prod_done{k}") for k in range(2)]
        conv_ps = [sem(f"conv_ps{k}") for k in range(2)]
        y_done = [sem(f"y_done{k}") for k in range(2)]
        QY = sb("QY", [P, DC, B, S])
        wstage = QY[:].rearrange("p c b s -> p (c b s)").rearrange("p (w c n) -> p w c n", w=4, c=DC)
        st1 = ExitStack()

        def sb1(name, shape, dt=F32):
            return st1.enter_context(nc.sbuf_tensor(name, shape, dt))
        WH = sb1("WH", [P, 4, DC, D], F32R)
        WL = sb1("WL", [P, 4, DC, D], F32R)
        qb = sb1("qb", [P, DC])
        kb = sb1("kb", [P, D])
        vb = sb1("vb", [P, D])
        ob = sb1("ob", [P, D])
        block = sb1("block", [P, P])
        headm = sb1("headm", [P, GPD])
        stt = [sb1(f"bn_stat{i}", [P, TPB, 6]) for i in range(2)]
        mv = [sb1(f"mean_var{i}", [P, TPB, 2]) for i in range(2)]
        ve = [sb1(f"var_eps{i}", [P, TPB]) for i in range(2)]
        rs = [sb1(f"rstd{i}", [P, TPB]) for i in range(2)]
        xn = [sb1(f"xn{i}", [P, TPB, D]) for i in range(2)]
        xTh = sb1("xTh", [P, DC, S], F32R)
        xTl = sb1("xTl", [P, DC, S], F32R)
        qE = sb1("qE", [P, DC, S])
        qR = sb1("qR", [P, DC, S])
        qpT = sb1("qpT", [P, DC, S])
        kt = sb1("kt", [P, TPB, D])
        kE = sb1("kE", [P, TPB, D])
        nqb = sb1("nqb", [P, DC])
        kp = sb1("kp", [P, TPB, D])
        v1 = sb1("v1", [P, TPB, DC, P + 1])
        KV = sb1("KV", [P, DC, P + GPD])
        dn = sb1("dn", [P, TPB * HEADS])
        rd = sb1("rd", [P, TPB * HEADS])
        at = sb1("at", [P, TPB, D])
        aTh = sb1("aTh", [P, DC, S], F32R)
        aTl = sb1("aTl", [P, DC, S], F32R)
        xo = xn[1]

        kpad = prod[0][:].rearrange("p c b n -> p (c b n)")[0:CH, 0:KPAD + 1]
        dsk = sb1("dsk", [CH, 1])
        ssm_in = sem("ssm_in")
        kpad_done, kpad_out = sem("kpad_done"), sem("kpad_out")
        tz_in = [sem(f"toeplitz_in{k}") for k in range(2)]
        c2_in = [sem(f"context_in{k}") for k in range(2)]
        consts_in = sem("consts_in")
        x_in = [sem(f"x_in{i}") for i in range(3)]
        w_in = [sem(f"w_in{i}") for i in range(4)]
        memsets = sem("memsets")
        w_hi = sem("w_hi")
        w_lo = sem("w_lo")
        ko_lo = sem("ko_lo")
        bn = [sem(f"ln{i}_bn") for i in range(2)]
        mvs = [sem(f"ln{i}_mv") for i in range(2)]
        ves = [sem(f"ln{i}_ve") for i in range(2)]
        rss = [sem(f"ln{i}_rstd") for i in range(2)]
        xns = [sem(f"ln{i}_xn") for i in range(2)]
        trs = [sem(f"ln{i}_transposed") for i in range(2)]
        xT_hi, xT_lo = sem("xT_hi"), sem("xT_lo")
        nqb_done, km_done = sem("nqb_done"), sem("km_done")
        q_ps, q_neg, q_act, qp_done = sem("q_ps"), sem("q_neg"), sem("q_act"), sem("qp_done")
        k_ps, kt_done, k_act, kp_done = sem("k_ps"), sem("kt_done"), sem("k_act"), sem("kp_done")
        v_ps, v_done = sem("v_ps"), sem("v_done")
        kv_ps, kv_done = sem("kv_ps"), sem("kv_done")
        att_ps, dn_done, rd_done, at_done = sem("att_ps"), sem("dn_done"), sem("rd_done"), sem("at_done")
        aT_ps, aT_hi, aT_lo = sem("aT_ps"), sem("aT_hi"), sem("aT_lo")
        o_ps, xo_done, x1_done = sem("o_ps"), sem("xo_done"), sem("x1_done")
        qy_done = sem("qy_done")

        block1 = nc.Block()
        block_ = block1.__enter__()

        def bcast_rows(v):
            return bass.AP(tensor=v.tensor, offset=0, ap=[[0, P], [1, D]])

        passed = {}

        def wait_apart(eng, semaphore, value):
            if eng.engine not in passed:
                passed[eng.engine] = sem(f"passed_{len(passed)}")
            eng.wait_ge(semaphore, value)
            eng.sem_inc(passed[eng.engine], 1)

        def load_toeplitz(sp, h, k):
            sp.dma_start(Tz[k][:], bass.AP(tensor=kpad_d.tensor, offset=h * (KPAD + 1), ap=[[1, P], [1, D]])
                         ).then_inc(tz_in[k], 16)

        def load_context(sp, h, k):
            sp.dma_start(C2[k][:], ctx2[h].rearrange("p c b j -> p (c b) j")).then_inc(c2_in[k], 16)

        def products(pool, i, k):
            pool.wait_ge(c2_in[k], 16 * (i + 1))
            pool.wait_ge(conv_ps[k], DC * i)
            o = prod[k][:].rearrange("p c b n -> p (c b) n")
            a = C2[k][:]
            shifted = bass.AP(tensor=a.tensor, offset=a.offset, ap=[a.ap[0], a.ap[1], [1, 4], [1, CD]])
            nc.gpsimd.tensor_tensor(o[:, :, 0:4 * CD].rearrange("p a (s j) -> p a s j", s=4),
                                    a[:, :, 0:CD].unsqueeze(2).broadcast_to([P, LB, 4, CD]), shifted,
                                    ALU.mult).then_inc(prod_done[k], 1)
            nc.gpsimd.tensor_tensor(o[:, :, 4 * CD:], a[:, :, 0:4], a[:, :, 4:8], ALU.mult).then_inc(prod_done[k], 1)

        def three_pass(pe, out_, lh, ll, rh, rl, first, last):
            pe.matmul(out_, lh, rh, start=first, stop=False)
            pe.matmul(out_, lh, rl, start=False, stop=False)
            return pe.matmul(out_, ll, rh, start=False, stop=last)

        def convolve(pe, i, k):
            pe.wait_ge(prod_done[k], 2 * (i + 1))
            pe.wait_ge(tz_in[k], 16 * (i + 1))
            pe.wait_ge(y_done[k], DC * i)
            for c in range(DC):
                for m in range(c + 1):
                    mm = pe.matmul(PS[:, DC * k + c, 0:B * NPAIR], Tz[k][:, (c - m) * P:(c - m + 1) * P],
                                   prod[k][:, m].rearrange("p b n -> p (b n)"), start=(m == 0), stop=(m == c))
                mm.then_inc(conv_ps[k], 1)

        @block_.sync
        def _(sp):
            def load_x(a, b, i):
                sp.dma_start(X[:, TPB * a:TPB * b], x[a:b].rearrange("b (t p) n -> p (b t) n", p=P)).then_inc(x_in[i], 16)

            def load_w(i, w):
                sp.dma_start(wstage[:, i], w.rearrange("(c p) n -> p c n", p=P)).then_inc(w_in[i], 16)

            load_x(0, 1, 0)
            sp.dma_start(ident[:], c_ident).then_inc(x_in[0], 16)
            load_w(0, qwT)
            load_w(1, kwT)
            sp.dma_start(qb[:], q_b).then_inc(consts_in, 16)
            sp.dma_start(kb[:], bcast_rows(k_b)).then_inc(consts_in, 16)
            sp.dma_start(vb[:], bcast_rows(v_b)).then_inc(consts_in, 16)
            sp.dma_start(ob[:], bcast_rows(o_b)).then_inc(consts_in, 16)
            sp.dma_start(block[:], c_block).then_inc(consts_in, 16)
            sp.dma_start(headm[:], c_head).then_inc(consts_in, 16)
            load_w(2, vwT)
            load_x(1, 2, 1)
            load_w(3, owT)
            load_x(2, B, 2)
            sp.wait_ge(memsets, 1)
            sp.dma_start(kpad[:, P - 1:KPAD], ssm).then_inc(ssm_in, 16)
            sp.dma_start(dsk[:], dskip).then_inc(ssm_in, 16)
            sp.wait_ge(kpad_done, 1)
            sp.dma_start(kpad_d, kpad[:]).then_inc(kpad_out, 16)
            sp.wait_ge(kpad_out, 16)
            for k in range(2):
                load_context(sp, k, k)
                load_toeplitz(sp, k, k)

        def rstd(pool, ln, b):
            wait_apart(pool, mvs[ln], TPB * (b + 1))
            nc.gpsimd.tensor_scalar(ve[ln][:], mv[ln][:, :, 1], LN_EPS, None, ALU.add).then_inc(ves[ln], 1)
            pool.wait_ge(ves[ln], b + 1)
            nc.gpsimd.tensor_tensor(rs[ln][:], ve[ln][:], nhalf[:], ALU.pow).then_inc(rss[ln], 1)

        @block_.gpsimd
        def _(pool):
            nc.gpsimd.memset(kpad[:], 0.0).then_inc(memsets, 1)
            nc.gpsimd.memset(nhalf[:], -0.5).then_inc(memsets, 1)
            nc.gpsimd.memset(v1[:, :, :, P:P + 1], 1.0).then_inc(memsets, 1)
            pool.wait_ge(memsets, 3)
            rstd(pool, 0, 0)
            pool.wait_ge(w_hi, 2)
            nc.gpsimd.tensor_tensor(WL[:, 1], wstage[:, 1], WH[:, 1].bitcast(F32), ALU.subtract).then_inc(ko_lo, 1)
            rstd(pool, 0, 1)
            pool.wait_ge(w_hi, 4)
            nc.gpsimd.tensor_tensor(WL[:, 3], wstage[:, 3], WH[:, 3].bitcast(F32), ALU.subtract).then_inc(ko_lo, 1)
            pool.wait_ge(ssm_in, 32)
            nc.gpsimd.tensor_tensor(kpad[:, P - 1:P], kpad[:, P - 1:P], dsk[:], ALU.add).then_inc(kpad_done, 1)
            with pool.Fori(1, B - 1) as b:
                rstd(pool, 0, b + 1)
                rstd(pool, 1, b - 1)
            rstd(pool, 1, B - 2)
            products(pool, 0, 0)
            rstd(pool, 1, B - 1)

        @block_.scalar
        def _(act):
            def split_hi(i):
                act.wait_ge(w_in[i], 16)
                act.activation(WH[:, i], wstage[:, i], ACT.Copy).then_inc(w_hi, 1)

            def x_hi(b):
                for t in range(TPB):
                    act.wait_ge(trs[0], TPB * b + t + 1)
                    act.activation(xTh[:, :, t * P:(t + 1) * P], PS[:, 6 + t].rearrange("p (c n) -> p c n", c=DC),
                                   ACT.Copy).then_inc(xT_hi, 1)

            def q_evac(b):
                for c in range(DC):
                    act.wait_ge(q_ps, DC * b + 2 * (c // 2) + 2)
                    ps = PS[:, 4 + c // 2, (c % 2) * S:(c % 2 + 1) * S]
                    act.activation(qE[:, c], ps, ACT.Relu, scale=-1.0, bias=nqb[:, c:c + 1]).then_inc(q_neg, 1)
                    act.activation(qR[:, c], ps, ACT.Relu, bias=qb[:, c:c + 1]).then_inc(q_act, 1)
                act.wait_ge(q_neg, DC * (b + 1))
                act.activation(qE[:], qE[:], ACT.Exp, scale=-1.0).then_inc(q_act, 1)

            def k_evac(b):
                for t in range(TPB):
                    act.wait_ge(km_done, TPB * b + t + 1)
                    act.activation(kE[:, t], kE[:, t], ACT.Exp).then_inc(k_act, 1)

            def a_hi(b):
                for t in range(TPB):
                    act.wait_ge(aT_ps, TPB * b + t + 1)
                    act.activation(aTh[:, :, t * P:(t + 1) * P], PS[:, 6 + t].rearrange("p (c n) -> p c n", c=DC),
                                   ACT.Copy).then_inc(aT_hi, 1)

            def qy_evac(b):
                for t in range(TPB):
                    wait_apart(act, trs[1], TPB * b + t + 1)
                    act.activation(QY[:, :, b, t * P:(t + 1) * P], PS[:, 6 + t].rearrange("p (c n) -> p c n", c=DC),
                                   ACT.Copy).then_inc(qy_done, 1)

            def step(b, first=False, last=False):
                q_evac(b)
                if not (isinstance(b, int) and b < 2):
                    qy_evac(b - 2)
                k_evac(b)
                if not first:
                    a_hi(b - 1)
                if not last:
                    x_hi(b + 1)

            split_hi(0)
            x_hi(0)
            for i in range(1, 4):
                split_hi(i)
            act.wait_ge(nqb_done, 1)
            step(0, first=True)
            step(1)
            with act.Fori(2, B - 1) as b:
                step(b)
            step(B - 1, last=True)
            qy_evac(B - 2)
            a_hi(B - 1)
            qy_evac(B - 1)

        @block_.vector
        def _(dve):
            def ln_stats(ln, b):
                for t in range(TPB):
                    if ln == 0:
                        i = b if isinstance(b, int) and b < 2 else 2
                        wait_apart(dve, x_in[i], 32 if i == 0 else 16)
                    else:
                        wait_apart(dve, x1_done, TPB * b + t + 1)
                    dve.bn_stats(stt[ln][:, t], X[:, TPB * b + t]).then_inc(bn[ln], 1)
                    wait_apart(dve, bn[ln], TPB * b + t + 1)
                    dve.bn_aggr(mv[ln][:, t], stt[ln][:, t]).then_inc(mvs[ln], 1)

            def ln_norm(ln, b):
                dve.wait_ge(rss[ln], b + 1)
                dve.wait_ge(trs[ln], TPB * b)
                for t in range(TPB):
                    dve.tensor_scalar(xn[ln][:, t], X[:, TPB * b + t], mv[ln][:, t, 0:1], rs[ln][:, t:t + 1],
                                      ALU.subtract, ALU.mult).then_inc(xns[ln], 1)

            def x_lo(b):
                for t in range(TPB):
                    dve.wait_ge(xT_hi, TPB * b + t + 1)
                    dve.tensor_tensor(xTl[:, :, t * P:(t + 1) * P], PS[:, 6 + t].rearrange("p (c n) -> p c n", c=DC),
                                      xTh[:, :, t * P:(t + 1) * P].bitcast(F32), ALU.subtract).then_inc(xT_lo, 1)

            def qp(b):
                dve.wait_ge(q_act, (DC + 1) * (b + 1))
                dve.tensor_tensor(qpT[:], qE[:], qR[:], ALU.add).then_inc(qp_done, 1)

            def k_bias(b):
                for t in range(TPB):
                    dve.wait_ge(k_ps, TPB * b + t + 1)
                    dve.tensor_tensor(kt[:, t], PS[:, t], kb[:], ALU.add).then_inc(kt_done, 1)
                for t in range(TPB):
                    dve.wait_ge(kt_done, TPB * b + t + 1)
                    dve.tensor_scalar(kE[:, t], kt[:, t], 0.0, None, ALU.min).then_inc(km_done, 1)

            def k_phi(b):
                for t in range(TPB):
                    dve.wait_ge(k_act, TPB * b + t + 1)
                    dve.scalar_tensor_tensor(out=kp[:, t], in0=kt[:, t], scalar=0.0, in1=kE[:, t], op0=ALU.max,
                                             op1=ALU.add).then_inc(kp_done, 1)

            def v_bias(b):
                for t in range(TPB):
                    dve.wait_ge(v_ps, TPB * b + t + 1)
                    dve.tensor_tensor(v1[:, t, :, 0:P], PS[:, 2 + t].rearrange("p (c n) -> p c n", c=DC),
                                      vb[:].rearrange("p (c n) -> p c n", c=DC), ALU.add).then_inc(v_done, 1)

            def kv_mask(b):
                dve.wait_ge(kv_ps, b + 1)
                for h in range(2):
                    ps = PS[:, 4 + h, 0:2 * (P + 1)].rearrange("p (c n) -> p c n", c=2)
                    dve.tensor_tensor(KV[:, 2 * h:2 * h + 2, 0:P], ps[:, :, 0:P],
                                      block[:].unsqueeze(1).broadcast_to([P, 2, P]), ALU.mult).then_inc(kv_done, 1)
                    dve.tensor_tensor(KV[:, 2 * h:2 * h + 2, P:], ps[:, :, P:P + 1].broadcast_to([P, 2, GPD]),
                                      headm[:].unsqueeze(1).broadcast_to([P, 2, GPD]), ALU.mult).then_inc(kv_done, 1)

            def att_norm(b):
                dve.wait_ge(att_ps, TPB * (b + 1))
                dve.tensor_scalar(dn[:].rearrange("p (k c h) -> p k c h", k=2 * TPB, c=2),
                                  PS[:, 0:2 * TPB, 0:2 * (P + GPD)].rearrange("p k (c n) -> p k c n", c=2)[:, :, :, P:],
                                  ATT_EPS, None, ALU.add).then_inc(dn_done, 1)
                dve.wait_ge(dn_done, b + 1)
                dve.reciprocal(rd[:], dn[:]).then_inc(rd_done, 1)
                dve.wait_ge(rd_done, b + 1)
                for k in range(2 * TPB):
                    half = at[:].rearrange("p t (k n) -> p (t k) n", k=2)[:, k]
                    dve.tensor_tensor(half.rearrange("p (c h n) -> p c h n", c=2, n=HD),
                                      PS[:, k, 0:2 * (P + GPD)].rearrange("p (c n) -> p c n", c=2)[:, :, 0:P]
                                      .rearrange("p c (h n) -> p c h n", n=HD),
                                      rd[:].rearrange("p (k c h) -> p k c h", c=2, h=GPD)[:, k].unsqueeze(3)
                                      .broadcast_to([P, 2, GPD, HD]), ALU.mult).then_inc(at_done, 1)

            def a_lo(b):
                for t in range(TPB):
                    dve.wait_ge(aT_hi, TPB * b + t + 1)
                    dve.tensor_tensor(aTl[:, :, t * P:(t + 1) * P], PS[:, 6 + t].rearrange("p (c n) -> p c n", c=DC),
                                      aTh[:, :, t * P:(t + 1) * P].bitcast(F32), ALU.subtract).then_inc(aT_lo, 1)

            def x_add(b):
                for t in range(TPB):
                    dve.wait_ge(o_ps, TPB * b + t + 1)
                    dve.tensor_tensor(xo[:, t], PS[:, 6 + t], ob[:], ALU.add).then_inc(xo_done, 1)
                for t in range(TPB):
                    dve.wait_ge(xo_done, TPB * b + t + 1)
                    dve.tensor_tensor(X[:, TPB * b + t], X[:, TPB * b + t], xo[:, t], ALU.add).then_inc(x1_done, 1)

            def step(b, first=False, last=False):
                if not first:
                    att_norm(b - 1)
                if not last:
                    ln_stats(0, b + 1)
                qp(b)
                if not last:
                    ln_norm(0, b + 1)
                k_bias(b)
                if not first:
                    a_lo(b - 1)
                k_phi(b)
                v_bias(b)
                if not first:
                    x_add(b - 1)
                kv_mask(b)
                if not last:
                    x_lo(b + 1)
                if not first:
                    ln_stats(1, b - 1)
                    ln_norm(1, b - 1)

            ln_stats(0, 0)
            ln_norm(0, 0)
            def w_lo_part(i):
                dve.wait_ge(w_hi, i + 1)
                dve.tensor_tensor(WL[:, i], wstage[:, i], WH[:, i].bitcast(F32), ALU.subtract).then_inc(w_lo, 1)

            w_lo_part(0)
            x_lo(0)
            dve.wait_ge(consts_in, 16 * 6)
            dve.tensor_scalar(nqb[:], qb[:], -1.0, None, ALU.mult).then_inc(nqb_done, 1)
            w_lo_part(2)
            dve.wait_ge(memsets, 3)
            step(0, first=True)
            step(1)
            with dve.Fori(2, B - 1) as b:
                step(b)
            step(B - 1, last=True)
            att_norm(B - 1)
            a_lo(B - 1)
            x_add(B - 1)
            ln_stats(1, B - 1)
            ln_norm(1, B - 1)

        @block_.tensor
        def _(pe):
            def transpose_tiles(src, banks, done):
                for t in range(TPB):
                    for c in range(DC):
                        last = pe.transpose(PS[:, banks + t, c * P:(c + 1) * P], src[:, t, c * P:(c + 1) * P], ident[:])
                    last.then_inc(done, 1)

            def t1(b):
                pe.wait_ge(xns[0], TPB * (b + 1))
                if not (isinstance(b, int) and b <= 1):
                    pe.wait_ge(xo_done, TPB * (b - 1))
                transpose_tiles(xn[0], 6, trs[0])

            def qproj(b):
                pe.wait_ge(xT_hi, TPB * (b + 1))
                pe.wait_ge(xT_lo, TPB * (b + 1))
                pe.wait_ge(kv_done, 4 * b)
                for c in range(DC):
                    o = PS[:, 4 + c // 2, (c % 2) * S:(c % 2 + 1) * S]
                    for hc in range(DC):
                        w = (0, hc, slice(c * P, (c + 1) * P))
                        mm = three_pass(pe, o, WH[(slice(None),) + w], WL[(slice(None),) + w], xTh[:, hc], xTl[:, hc],
                                        hc == 0, hc == DC - 1)
                    mm.then_inc(q_ps, 1)

            def token_proj(i, srch, srcl, bank, done):
                for t in range(TPB):
                    for c in range(DC):
                        ts = slice(t * P, (t + 1) * P)
                        mm = three_pass(pe, PS[:, bank + t], srch[:, c, ts], srcl[:, c, ts], WH[:, i, c], WL[:, i, c],
                                        c == 0, c == DC - 1)
                    mm.then_inc(done, 1)

            def att_t(b):
                pe.wait_ge(at_done, 2 * TPB * (b + 1))
                pe.wait_ge(qy_done, TPB * b)
                transpose_tiles(at, 6, aT_ps)

            def oproj(b):
                pe.wait_ge(aT_hi, TPB * (b + 1))
                pe.wait_ge(aT_lo, TPB * (b + 1))
                token_proj(3, aTh, aTl, 6, o_ps)

            def kv(b):
                pe.wait_ge(kp_done, TPB * (b + 1))
                pe.wait_ge(v_done, TPB * (b + 1))
                pe.wait_ge(q_act, (DC + 1) * (b + 1))
                for c in range(DC):
                    o = PS[:, 4 + c // 2, (c % 2) * (P + 1):(c % 2 + 1) * (P + 1)]
                    for t in range(TPB):
                        mm = pe.matmul(o, kp[:, t, c * P:(c + 1) * P], v1[:, t, c], start=(t == 0), stop=(t == TPB - 1))
                mm.then_inc(kv_ps, 1)

            def att(b):
                pe.wait_ge(kv_done, 4 * (b + 1))
                pe.wait_ge(qp_done, b + 1)
                for t in range(TPB):
                    for c in range(DC):
                        o = PS[:, 2 * t + c // 2, (c % 2) * (P + GPD):(c % 2 + 1) * (P + GPD)]
                        mm = pe.matmul(o, qpT[:, c, t * P:(t + 1) * P], KV[:, c], start=True, stop=True)
                    mm.then_inc(att_ps, 1)

            def t2(b):
                pe.wait_ge(xns[1], TPB * (b + 1))
                pe.wait_ge(xo_done, TPB * (b + 1))
                pe.wait_ge(xT_lo, TPB * (b + 3) if not isinstance(b, int) else TPB * min(b + 3, B))
                transpose_tiles(xn[1], 6, trs[1])

            def step(b, first=False, last=False):
                qproj(b)
                if not (isinstance(b, int) and b < 2):
                    t2(b - 2)
                pe.wait_ge(ko_lo, 1)
                pe.wait_ge(at_done, 2 * TPB * b)
                token_proj(1, xTh, xTl, 0, k_ps)
                if not first:
                    att_t(b - 1)
                pe.wait_ge(w_lo, 2)
                token_proj(2, xTh, xTl, 2, v_ps)
                if not first:
                    pe.wait_ge(ko_lo, 2)
                    oproj(b - 1)
                kv(b)
                if not last:
                    t1(b + 1)
                att(b)

            pe.wait_ge(x_in[0], 32)
            t1(0)
            pe.wait_ge(w_hi, 1)
            pe.wait_ge(w_lo, 1)
            step(0, first=True)
            step(1)
            with pe.Fori(2, B - 1) as b:
                step(b)
            step(B - 1, last=True)
            t2(B - 2)
            att_t(B - 1)
            oproj(B - 1)
            pe.wait_ge(at_done, 2 * TPB * B)
            convolve(pe, 0, 0)
            t2(B - 1)
        block1.__exit__(None, None, None)
        st1.close()
        ws = [sb(f"ws{w}", [P, DC + IC, D]) for w in range(2)]
        wh = [sb(f"wh{w}", [P, DC + IC, D], F32R) for w in range(2)]
        wl = [sb(f"wl{w}", [P, DC + IC, D], F32R) for w in range(2)]
        ws_in = [sem(f"ws_in{w}") for w in range(2)]
        gw = sb("gw", [P, DC, NE])
        gw_hl = sb("gw_hl", [P, DC, 2, NE], F32R)
        zrow = sb("zrow", [P, D])
        gw_in, zero_out = sem("gw_in"), sem("zero_out")
        fixed_hi, fixed_lo = sem("fixed_hi"), sem("fixed_lo")

        def load_expert(sp, e, w):
            sp.dma_start(ws[w][:, 0:DC], gu_w[e]).then_inc(ws_in[w], 16)
            sp.dma_start(ws[w][:, DC:], dn_w[e]).then_inc(ws_in[w], 16)

        st2 = ExitStack()

        def sb2(name, shape, dt=F32):
            return st2.enter_context(nc.sbuf_tensor(name, shape, dt))
        prod.append(sb2("prod1", [P, DC, B, NPAIR]))
        Q2 = [sb2(f"Q2{k}", [P, LB, 2 * CD]) for k in range(2)]
        Y = [sb2(f"Y{k}", [P, LB, NPAIR]) for k in range(2)]
        term = [sb2(f"term{k}", [P, LB, CD, CD]) for k in range(2)]
        q2_done = [sem(f"q2_done{k}") for k in range(2)]
        term_dve = [sem(f"term_dve{k}") for k in range(2)]
        term_pool = [sem(f"term_pool{k}") for k in range(2)]
        reduced = [sem(f"reduced{k}") for k in range(2)]
        NM = 7
        QYh = QY[:].rearrange("p c b s -> p (c b) s")

        with nc.Block() as block_:
            @block_.sync
            def _(sp):
                load_expert(sp, NE, 1)
                sp.dma_start(gw[:], gateT.rearrange("(c p) n -> p c n", p=P)).then_inc(gw_in, 16)
                sp.wait_ge(memsets, 4)
                for t in range(SLOT_T):
                    rows = slice(B * S + t * P, B * S + (t + 1) * P)
                    sp.dma_start(xs_d[rows], zrow[:]).then_inc(zero_out, 16)
                    sp.dma_start(out[rows], zrow[:]).then_inc(zero_out, 16)

                def next_heads(i, last=False):
                    sp.wait_ge(prod_done[1], 2 * (i + 1))
                    load_context(sp, 2 * i + 3, 1)
                    sp.wait_ge(conv_ps[0], DC * (i + 1))
                    load_toeplitz(sp, 2 * i + 2, 0)
                    if not last:
                        sp.wait_ge(prod_done[0], 2 * (i + 2))
                        load_context(sp, 2 * i + 4, 0)
                    sp.wait_ge(conv_ps[1], DC * (i + 1))
                    load_toeplitz(sp, 2 * i + 3, 1)

                sp.wait_ge(prod_done[0], 2)
                load_context(sp, 2, 0)
                with sp.Fori(0, CH // 2 - 2) as i:
                    next_heads(i)
                next_heads(CH // 2 - 2, last=True)
            @block_.gpsimd
            def _(pool):
                def half_term(i, k):
                    pool.wait_ge(y_done[k], DC * (i + 1))
                    pool.wait_ge(q2_done[k], i + 1)
                    pool.wait_ge(reduced[k], i)
                    nc.gpsimd.tensor_tensor(term[k][:, :, 7].rearrange("p a (t j) -> p a t j", t=2),
                                            Y[k][:, :, 4 * CD:].unsqueeze(2).broadcast_to([P, LB, 2, 4]),
                                            Q2[k][:, :, 4:12].rearrange("p a (t j) -> p a t j", t=2),
                                            ALU.mult).then_inc(term_pool[k], 1)

                nc.gpsimd.memset(zrow[:], 0.0).then_inc(memsets, 1)
                def pair_of_heads(i):
                    products(pool, i, 1)
                    half_term(i, 0)
                    products(pool, i + 1, 0)
                    half_term(i, 1)

                products(pool, 0, 1)
                half_term(0, 0)
                products(pool, 1, 0)
                half_term(0, 1)
                with pool.Fori(1, CH // 2 - 1) as i:
                    pair_of_heads(i)
                def shared_lo(a, b):
                    nc.gpsimd.tensor_tensor(wl[1][:, a:b], ws[1][:, a:b], wh[1][:, a:b].bitcast(F32), ALU.subtract
                                            ).then_inc(fixed_lo, 1)

                pool.wait_ge(fixed_hi, 2)
                nc.gpsimd.tensor_tensor(gw_hl[:, :, 1], gw[:], gw_hl[:, :, 0].bitcast(F32), ALU.subtract).then_inc(fixed_lo, 1)
                products(pool, CH // 2 - 1, 1)
                shared_lo(0, 3)
                half_term(CH // 2 - 1, 0)
                shared_lo(3, DC + IC)
                half_term(CH // 2 - 1, 1)

            @block_.scalar
            def _(act):
                def pair_of_heads(i):
                    for k in range(2):
                        wait_apart(act, reduced[k], i)
                        act.activation(Q2[k][:].rearrange("p a (t j) -> p a t j", t=2),
                                       QYh[:, :, bass.ds((2 * i + k) * CD, CD)].unsqueeze(2).broadcast_to([P, LB, 2, CD]),
                                       ACT.Copy).then_inc(q2_done[k], 1)
                        for c in range(DC):
                            act.wait_ge(conv_ps[k], DC * i + c + 1)
                            act.activation(Y[k][:, c * B:(c + 1) * B].rearrange("p b n -> p (b n)"),
                                           PS[:, DC * k + c, 0:B * NPAIR], ACT.Copy).then_inc(y_done[k], 1)

                pair_of_heads(0)
                act.wait_ge(gw_in, 16)
                act.activation(gw_hl[:, :, 0], gw[:], ACT.Copy).then_inc(fixed_hi, 1)
                act.wait_ge(ws_in[1], 32)
                act.activation(wh[1][:], ws[1][:], ACT.Copy).then_inc(fixed_hi, 1)
                with act.Fori(1, CH // 2) as i:
                    pair_of_heads(i)

            @block_.vector
            def _(dve):
                def terms(i, k):
                    dve.wait_ge(y_done[k], DC * (i + 1))
                    dve.wait_ge(q2_done[k], i + 1)
                    y, q, t = Y[k][:], Q2[k][:], term[k]
                    shifted = bass.AP(tensor=q.tensor, offset=q.offset, ap=[q.ap[0], q.ap[1], [1, 4], [1, CD]])
                    dve.tensor_tensor(t[:, :, 0:4], y[:, :, 0:4 * CD].rearrange("p a (s j) -> p a s j", s=4),
                                      shifted, ALU.mult).then_inc(term_dve[k], 1)
                    for r in range(1, 4):
                        dve.tensor_tensor(t[:, :, 3 + r, r:CD], y[:, :, r * CD:(r + 1) * CD - r], q[:, :, 0:CD - r],
                                          ALU.mult).then_inc(term_dve[k], 1)
                        dve.tensor_tensor(t[:, :, 3 + r, 0:r], y[:, :, (r + 1) * CD - r:(r + 1) * CD], q[:, :, CD - r:CD],
                                          ALU.mult).then_inc(term_dve[k], 1)

                def reduce(i, k):
                    dve.wait_ge(term_dve[k], NM * (i + 1))
                    wait_apart(dve, term_pool[k], i + 1)
                    dve.tensor_reduce(QYh[:, :, bass.ds((2 * i + k) * CD, CD)],
                                      term[k][:].rearrange("p a s m -> p a m s"), AX_X, ALU.add).then_inc(reduced[k], 1)

                with dve.Fori(0, CH // 2) as i:
                    for k in range(2):
                        terms(i, k)
                        reduce(i, k)

            @block_.tensor
            def _(pe):
                convolve(pe, 0, 1)
                with pe.Fori(1, CH // 2) as i:
                    for k in range(2):
                        convolve(pe, i, k)
        st2.close()
        x3h = [sb(f"x3h{p}", [P, DC, P], F32R) for p in range(2)]
        x3l = [sb(f"x3l{p}", [P, DC, P], F32R) for p in range(2)]
        sg = [sb(f"sg{p}", [P, I_FF]) for p in range(2)]
        hh = [sb(f"hh{p}", [P, I_FF]) for p in range(2)]
        hTh = [sb(f"hTh{p}", [P, IC, P], F32R) for p in range(2)]
        hTl = [sb(f"hTl{p}", [P, IC, P], F32R) for p in range(2)]
        LG = sb("LG", [P, NT, NE])
        table_row = sb("table_row", [P, 1])
        eb = sb("eb", [P, NE])
        lt4 = sb("lt4", [P, 4, 4])
        tri = sb("tri", [P, P])
        free = sb("free", [P, P])
        slotk = sb("slotk", [P, B * S // SLOT])
        tok = sb("tok", [P, NT + SLOT_T])
        r_in = sem("r_in")
        st3 = ExitStack()

        def sb3(name, shape, dt=F32):
            return st3.enter_context(nc.sbuf_tensor(name, shape, dt))
        ysl = [sb3(f"ysl{p}", [P, DC, P]) for p in range(2)]
        xn3 = [sb3(f"xn3{p}", [P, D]) for p in range(2)]
        bst3 = [sb3(f"bn_stat3{p}", [P, 6]) for p in range(2)]
        mv3 = [sb3(f"mean_var3{p}", [P, 2]) for p in range(2)]
        ve3 = [sb3(f"var_eps3{p}", [P, 1]) for p in range(2)]
        rs3 = [sb3(f"rstd3{p}", [P, 1]) for p in range(2)]

        def pair(name):
            return [sem(f"{name}{p}") for p in range(2)]
        ysl_done, t3_ps, x2_done, bn3, mv3s, ve3s, rs3s, xn3_done = (
            pair(n) for n in ("ysl_done", "t3_ps", "x2_done", "ln2_bn", "ln2_mv", "ln2_ve", "ln2_rstd", "ln2_xn"))
        xs_out, t4_ps, x3_hi, x3_lo, rt_ps, lg_done, gu_ps, silu_done, h_done = (
            pair(n) for n in ("xs_out", "t4_ps", "x3_hi", "x3_lo", "rt_ps", "lg_done", "gu_ps", "silu_done", "h_done"))
        t5_ps, h_hi, h_lo, dn_ps, x3_done = (pair(n) for n in ("t5_ps", "h_hi", "h_lo", "dn_ps", "x3_done"))
        x3_out = sem("x3_out")

        def bank_chunks(bank, c=DC):
            return PS[:, bank, 0:c * P].rearrange("p (c n) -> p c n", c=c)

        def gate_up(pe, p, w, done):
            for c in range(DC):
                mm = three_pass(pe, PS[:, 3 + p], x3h[p][:, c], x3l[p][:, c], wh[w][:, c], wl[w][:, c], c == 0, c == DC - 1)
            mm.then_inc(done, 1)

        def down(pe, p, w, done):
            for c in range(IC):
                mm = three_pass(pe, PS[:, 6 + p], hTh[p][:, c], hTl[p][:, c], wh[w][:, DC + c], wl[w][:, DC + c],
                                c == 0, c == IC - 1)
            mm.then_inc(done, 1)

        with nc.Block() as block_:
            @block_.sync
            def _(sp):
                sp.dma_start(eb[:], bass.AP(tensor=ebias.tensor, offset=0, ap=[[0, P], [1, NE]])).then_inc(r_in, 16)
                for dst, src in ((lt4, c_lt4), (tri, c_tri), (free, c_free), (slotk, c_slotk), (tok, c_tok)):
                    sp.dma_start(dst[:], src).then_inc(r_in, 16)

                def store_xn(i, p):
                    sp.wait_ge(xn3_done[p], i + 1)
                    sp.dma_start(xs_d[bass.ds((TPB * i + p) * P, P)], xn3[p][:]).then_inc(xs_out[p], 16)

                def store_x(i, p):
                    sp.wait_ge(x3_done[p], i + 1)
                    sp.dma_start(out[bass.ds((TPB * i + p) * P, P)], X[:, TPB * i + p]).then_inc(x3_out, 16)

                store_xn(0, 0)
                store_xn(0, 1)
                with sp.Fori(0, B - 1) as i:
                    for p in range(2):
                        store_xn(i + 1, p)
                        store_x(i, p)
                store_x(B - 1, 0)
                store_x(B - 1, 1)
                for p in range(2):
                    sp.wait_ge(xs_out[p], 16 * B)

            @block_.gpsimd
            def _(pool):
                def rstd3(i, p):
                    wait_apart(pool, mv3s[p], i + 1)
                    nc.gpsimd.tensor_scalar(ve3[p][:], mv3[p][:, 1:2], LN_EPS, None, ALU.add).then_inc(ve3s[p], 1)
                    pool.wait_ge(ve3s[p], i + 1)
                    nc.gpsimd.tensor_tensor(rs3[p][:], ve3[p][:], nhalf[:, 0:1], ALU.pow).then_inc(rs3s[p], 1)

                with pool.Fori(0, B) as i:
                    for p in range(2):
                        rstd3(i, p)

            @block_.scalar
            def _(act):
                def stage_y(i, p, first=False):
                    if not first:
                        wait_apart(act, t3_ps[p], i)
                    act.activation(ysl[p][:], QY[:, :, i, p * P:(p + 1) * P], ACT.Copy).then_inc(ysl_done[p], 1)

                def x_hi(i, p):
                    act.wait_ge(t4_ps[p], i + 1)
                    act.activation(x3h[p][:], bank_chunks(1), ACT.Copy).then_inc(x3_hi[p], 1)

                def silu(i, p):
                    act.wait_ge(gu_ps[p], i + 1)
                    act.activation(sg[p][:], PS[:, 3 + p, 0:I_FF], ACT.Silu).then_inc(silu_done[p], 1)

                def hid_hi(i, p):
                    act.wait_ge(t5_ps[p], i + 1)
                    act.activation(hTh[p][:], bank_chunks(5, IC), ACT.Copy).then_inc(h_hi[p], 1)

                def step(i, p, last=False):
                    if not last or p == 0:
                        x_hi(i + p, 1 - p)
                    silu(i, p)
                    if not last and not (p == 1 and isinstance(i, int) and i == B - 2):
                        stage_y(i + 1 + p, 1 - p)
                    hid_hi(i, p)

                stage_y(0, 0, first=True)
                stage_y(0, 1, first=True)
                act.activation(table_row[:], ident[:, 0:1], ACT.Silu)
                stage_y(1, 0)
                x_hi(0, 0)
                with act.Fori(0, B - 2) as i:
                    for p in range(2):
                        step(i, p)
                step(B - 2, 0)
                step(B - 2, 1)
                step(B - 1, 0, last=True)
                step(B - 1, 1, last=True)

            @block_.vector
            def _(dve):
                def x2(i, p):
                    dve.wait_ge(t3_ps[p], i + 1)
                    dve.tensor_tensor(X[:, TPB * i + p], X[:, TPB * i + p], PS[:, 0], ALU.add).then_inc(x2_done[p], 1)
                    wait_apart(dve, x2_done[p], i + 1)
                    dve.bn_stats(bst3[p][:], X[:, TPB * i + p]).then_inc(bn3[p], 1)
                    wait_apart(dve, bn3[p], i + 1)
                    dve.bn_aggr(mv3[p][:], bst3[p][:]).then_inc(mv3s[p], 1)

                def norm(i, p):
                    dve.wait_ge(xs_out[p], 16 * i)
                    dve.wait_ge(t4_ps[p], i)
                    dve.wait_ge(rs3s[p], i + 1)
                    dve.tensor_scalar(xn3[p][:], X[:, TPB * i + p], mv3[p][:, 0:1], rs3[p][:], ALU.subtract,
                                      ALU.mult).then_inc(xn3_done[p], 1)

                def x_lo(i, p):
                    dve.wait_ge(x3_hi[p], i + 1)
                    dve.tensor_tensor(x3l[p][:], bank_chunks(1), x3h[p][:].bitcast(F32), ALU.subtract).then_inc(x3_lo[p], 1)

                def hidden(i, p):
                    dve.wait_ge(silu_done[p], i + 1)
                    dve.tensor_tensor(hh[p][:], PS[:, 3 + p, I_FF:2 * I_FF], sg[p][:], ALU.mult).then_inc(h_done[p], 1)

                def logits(i, p):
                    wait_apart(dve, rt_ps[p], i + 1)
                    dve.tensor_reduce(LG[:, TPB * i + p], PS[:, 2, 0:2 * NE].rearrange("p (a e) -> p e a", a=2), AX_X, ALU.add
                                      ).then_inc(lg_done[p], 1)

                def hid_lo(i, p):
                    dve.wait_ge(h_hi[p], i + 1)
                    dve.tensor_tensor(hTl[p][:], bank_chunks(5, IC), hTh[p][:].bitcast(F32), ALU.subtract).then_inc(h_lo[p], 1)

                def add_shared(i, p):
                    dve.wait_ge(dn_ps[p], i + 1)
                    dve.tensor_tensor(X[:, TPB * i + p], X[:, TPB * i + p], PS[:, 6 + p], ALU.add).then_inc(x3_done[p], 1)

                def step(i, p, first=False, last=False):
                    if not last or p == 0:
                        x_lo(i + p, 1 - p)
                    if not last:
                        x2(i + 1, p)
                    hidden(i, p)
                    if not last:
                        norm(i + 1, p)
                    logits(i, p)
                    if not first:
                        add_shared(i + p - 1, 1 - p)
                    hid_lo(i, p)

                x2(0, 0)
                norm(0, 0)
                x2(0, 1)
                x_lo(0, 0)
                norm(0, 1)
                step(0, 0, first=True)
                step(0, 1)
                step(1, 0)
                step(1, 1)
                with dve.Fori(2, B - 1) as i:
                    for p in range(2):
                        step(i, p)
                step(B - 1, 0, last=True)
                step(B - 1, 1, last=True)
                add_shared(B - 1, 1)

            @block_.tensor
            def _(pe):
                def t3(i, p, before):
                    pe.wait_ge(ysl_done[p], i + 1)
                    pe.wait_ge(x2_done[1 - p], before)
                    for c in range(DC):
                        mm = pe.transpose(PS[:, 0, c * P:(c + 1) * P], ysl[p][:, c], ident[:])
                    mm.then_inc(t3_ps[p], 1)

                def t4(i, p, before):
                    pe.wait_ge(xn3_done[p], i + 1)
                    pe.wait_ge(x3_lo[1 - p], before)
                    for c in range(DC):
                        mm = pe.transpose(PS[:, 1, c * P:(c + 1) * P], xn3[p][:, c * P:(c + 1) * P], ident[:])
                    mm.then_inc(t4_ps[p], 1)

                def router(i, p, before):
                    pe.wait_ge(lg_done[1 - p], before)
                    for c in range(DC):
                        both = gw_hl[:, c].rearrange("p a e -> p (a e)")
                        pe.matmul(PS[:, 2, 0:2 * NE], x3h[p][:, c], both, start=(c == 0), stop=False)
                        mm = pe.matmul(PS[:, 2, 0:2 * NE], x3l[p][:, c], both, start=False, stop=(c == DC - 1))
                    mm.then_inc(rt_ps[p], 1)

                def t5(i, p, before):
                    pe.wait_ge(h_done[p], i + 1)
                    pe.wait_ge(h_lo[1 - p], before)
                    for c in range(IC):
                        mm = pe.transpose(PS[:, 5, c * P:(c + 1) * P], hh[p][:, c * P:(c + 1) * P], ident[:])
                    mm.then_inc(t5_ps[p], 1)

                def step(i, p, first=False, last=False):
                    if not last or p == 0:
                        t4(i + p, 1 - p, i + 1)
                    if not last:
                        t3(i + 1, p, i + p + 1)
                    pe.wait_ge(x3_lo[p], i + 1)
                    pe.wait_ge(h_done[p], i)
                    gate_up(pe, p, 1, gu_ps[p])
                    router(i, p, i + p)
                    if not first:
                        pe.wait_ge(h_lo[1 - p], i + p)
                        pe.wait_ge(x3_done[1 - p], i + p - 1)
                        down(pe, 1 - p, 1, dn_ps[1 - p])
                    t5(i, p, i + p)

                t3(0, 0, 0)
                t3(0, 1, 1)
                t4(0, 0, 0)
                step(0, 0, first=True)
                step(0, 1)
                step(1, 0)
                step(1, 1)
                with pe.Fori(2, B - 1) as i:
                    for p in range(2):
                        step(i, p)
                step(B - 1, 0, last=True)
                step(B - 1, 1, last=True)
                pe.wait_ge(h_lo[1], B)
                pe.wait_ge(x3_done[1], B - 1)
                down(pe, 1, 1, dn_ps[1])
        st3.close()
        W4 = sb("W4", [P, NT, TOPK])
        IDX = sb("IDX", [P, NCOL], U32)
        WPOS = sb("WPOS", [P, NCOL])
        ES = sb("ES", [P, NSLOT], I32)
        MORE = sb("MORE", [P, 1], I32)
        st4 = ExitStack()

        def sb4(name, shape, dt=F32):
            return st4.enter_context(nc.sbuf_tensor(name, shape, dt))
        ones = sb4("ones", [P, P])
        SC = sb4("SC", [P, NT, NE])
        BI = sb4("BI", [P, NT, NE])
        MB = sb4("MB", [P, NT, NE])
        g_hi, g_lo = sb4("g_hi", [P, NT * 4, 2]), sb4("g_lo", [P, NT * 4, 2])
        g_a, g_b, g_c, GS = (sb4(n, [P, NT * 4]) for n in ("g_a", "g_b", "g_c", "GS"))
        g_gt, g_eq = sb4("g_gt", [P, NT, 4, 4]), sb4("g_eq", [P, NT, 4, 4])
        V8 = sb4("V8", [P, NT, 8])
        I8 = sb4("I8", [P, NT, 8], U32)
        EF = sb4("EF", [P, NT, TOPK])
        OH = sb4("OH", [P, NT, TOPK, NE])
        OT = sb4("OT", [P, NT, TOPK, NE])
        WS = sb4("WS", [P, NT, TOPK])
        dsum, drec = sb4("dsum", [P, NT]), sb4("drec", [P, NT])
        SEL = sb4("SEL", [P, NT, NE])
        TOT = sb4("TOT", [P, NT, NE])
        acc = [sb4(f"acc{i}", [P, NT, NE]) for i in range(2)]
        NSK = sb4("NSK", [P, NE, B * S // SLOT])
        NS = sb4("NS", [P, NE])
        se = [sb4(f"se{i}", [P, NE]) for i in range(2)]
        base = sb4("base", [P, NE])
        POS = sb4("POS", [P, NT, NE])
        DEST = sb4("DEST", [P, NT, TOPK])
        DI, LOWI, HII = (sb4(n, [P, NT, TOPK], I32) for n in ("DI", "LOWI", "HII"))
        LOW, HIF, TOKV = (sb4(n, [P, NT, TOPK]) for n in ("LOW", "HIF", "TOKV"))
        LAST = sb4("LAST", [P, 1], I32)
        SLE = sb4("SLE", [P, NSLOT, NE])
        ESF = sb4("ESF", [P, NSLOT])
        HOT = 4
        hot_rows = QY[:].rearrange("p c b s -> p (c b s)")

        def in_qy(start, n):
            return [hot_rows[:, start + p * TOPK * n:start + (p + 1) * TOPK * n].rearrange("p (r n) -> p r n", n=n)
                    for p in range(HOT)]
        lowhot = in_qy(0, P)
        colone = in_qy(HOT * TOPK * P, NCOL)
        colhot = [h.rearrange("p r (a n) -> p r a n", a=2)
                  for h in in_qy(HOT * TOPK * (P + NCOL), 2 * NCOL)]
        score_done, chain = sem("score_done"), sem("route_step")
        sel_done, count_ps = sem("sel_done"), sem("count_ps")
        one_hot, token_hot, weight_hot, hot_used = sem("one_hot"), sem("token_hot"), sem("weight_hot"), sem("hot_used")

        w5_hi, w5_lo, w5_lop, ws5_in = pair("w5_hi"), pair("w5_lo"), pair("w5_lop"), pair("ws5_in")
        es_done = sem("es_done")
        HALVES = ((0, 3), (3, DC + IC))

        def load_slot(sp, slot, w):
            e = sp.value_load(ES[0:1, bass.ds(slot, 1)], min_val=0, max_val=NE - 1)
            sp.dma_start(ws[w][:, 0:DC], gu_w[bass.ds(e, 1)].rearrange("o p c n -> p (o c) n")).then_inc(ws5_in[w], 16)
            sp.dma_start(ws[w][:, DC:], dn_w[bass.ds(e, 1)].rearrange("o p c n -> p (o c) n")).then_inc(ws5_in[w], 16)

        def w_hi_part(act, i, w, half):
            a, b = HALVES[half]
            act.wait_ge(ws5_in[w], 32 * (i + 1))
            act.activation(wh[w][:, a:b], ws[w][:, a:b], ACT.Copy).then_inc(w5_hi[w], 1)

        def w_lo_part(dve, i, w, half):
            a, b = HALVES[half]
            dve.wait_ge(w5_hi[w], 2 * i + half + 1)
            dve.tensor_tensor(wl[w][:, a:b - 1], ws[w][:, a:b - 1], wh[w][:, a:b - 1].bitcast(F32), ALU.subtract
                              ).then_inc(w5_lo[w], 1)

        def w_lo_pool(pool, i, w, half):
            c = HALVES[half][1] - 1
            pool.wait_ge(w5_hi[w], 2 * i + half + 1)
            nc.gpsimd.tensor_tensor(wl[w][:, c], ws[w][:, c], wh[w][:, c].bitcast(F32), ALU.subtract
                                    ).then_inc(w5_lop[w], 1)

        with nc.Block() as block_:
            @block_.sync
            def _(sp):
                sp.wait_ge(es_done, 1)
                load_slot(sp, 0, 0)
                load_slot(sp, 1, 1)
                sp.wait_ge(x3_out, 16 * NT)
                sp.wait_ge(zero_out, 32 * SLOT_T)

            @block_.scalar
            def _(act):
                act.activation(SC[:], LG[:], ACT.Sigmoid).then_inc(score_done, 1)
                act.activation(table_row[:], ident[:, 0:1], ACT.Silu)
                def weight_one_hots(i, p, first=False):
                    t = HOT * i + p
                    wait_apart(act, one_hot, 2 * t + 1)
                    if not first:
                        wait_apart(act, hot_used, t - HOT + 1)
                    for r in range(TOPK):
                        act.activation(colhot[p][:, r, 1], colone[p][:, r], ACT.Copy, scale=W4[:, t, r:r + 1]
                                       ).then_inc(weight_hot, 1)

                for p in range(HOT):
                    weight_one_hots(0, p, first=True)
                with act.Fori(1, NT // HOT) as i:
                    for p in range(HOT):
                        weight_one_hots(i, p)

            @block_.tensor
            def _(pe):
                pe.wait_ge(sel_done, 1)
                pe.wait_ge(r_in, 16 * 6)
                pe.wait_ge(memsets, 5)
                sel = SEL[:].rearrange("p t e -> p (t e)")
                pe.matmul(PS[:, 0, 0:NT * NE], tri[:], sel, start=True, stop=True)
                pe.matmul(PS[:, 1, 0:NT * NE], ones[:], sel, start=True, stop=True).then_inc(count_ps, 1)

                def place(i, p, first=False, last=False):
                    t = HOT * i + p
                    pe.wait_ge(one_hot, 2 * (t + 1))
                    pe.wait_ge(token_hot, t + 1)
                    pe.wait_ge(weight_hot, TOPK * (t + 1))
                    for r in range(TOPK):
                        mm = pe.matmul(PS[:, 2, 0:2 * NCOL], lowhot[p][:, r], colhot[p][:, r].rearrange("p a c -> p (a c)"),
                                       start=(first and r == 0), stop=(last and r == TOPK - 1))
                    mm.then_inc(hot_used, 1)

                for p in range(HOT):
                    place(0, p, first=(p == 0))
                with pe.Fori(1, NT // HOT - 1) as i:
                    for p in range(HOT):
                        place(i, p)
                for p in range(HOT):
                    place(NT // HOT - 1, p, last=(p == HOT - 1))

            @block_.gpsimd
            def _(pool):
                nc.gpsimd.memset(ones[:], 1.0).then_inc(memsets, 1)

                def token_one_hots(i, p, first=False):
                    t = HOT * i + p
                    wait_apart(pool, one_hot, 2 * t + 1)
                    if not first:
                        wait_apart(pool, hot_used, t - HOT + 1)
                    nc.gpsimd.tensor_tensor(colhot[p][:, :, 0], colone[p], TOKV[:, t].unsqueeze(2).broadcast_to([P, TOPK, NCOL]),
                                            ALU.mult).then_inc(token_hot, 1)

                for p in range(HOT):
                    token_one_hots(0, p, first=True)
                with pool.Fori(1, NT // HOT) as i:
                    for p in range(HOT):
                        token_one_hots(i, p)

            @block_.vector
            def _(dve):
                steps = [0]

                def link(ins):
                    steps[0] += 1
                    ins.then_inc(chain, 1)
                    dve.wait_ge(chain, steps[0])

                def post(ins):
                    steps[0] += 1
                    ins.then_inc(chain, 1)

                def tt(o, a, b, op):
                    link(dve.tensor_tensor(o, a, b, op))

                def tt_post(o, a, b, op):
                    post(dve.tensor_tensor(o, a, b, op))

                def reduce(o, a):
                    link(dve.tensor_reduce(o, a, AX_X, ALU.add))

                dve.wait_ge(r_in, 16 * 6)
                dve.wait_ge(score_done, 1)
                tt(BI[:], SC[:], eb[:].unsqueeze(1).broadcast_to([P, NT, NE]), ALU.add)
                quad = BI[:].rearrange("p t (g k) -> p (t g) k", k=4)
                tt_post(g_hi[:], quad[:, :, 0:4:2], quad[:, :, 1:4:2], ALU.max)
                tt(g_lo[:], quad[:, :, 0:4:2], quad[:, :, 1:4:2], ALU.min)
                tt_post(g_a[:], g_hi[:, :, 0], g_hi[:, :, 1], ALU.max)
                tt_post(g_b[:], g_hi[:, :, 0], g_hi[:, :, 1], ALU.min)
                tt(g_c[:], g_lo[:, :, 0], g_lo[:, :, 1], ALU.max)
                tt(g_b[:], g_b[:], g_c[:], ALU.max)
                tt(GS[:], g_a[:], g_b[:], ALU.add)
                gs = GS[:].rearrange("p (t g) -> p t g", g=4)
                other = gs.unsqueeze(2).broadcast_to([P, NT, 4, 4])
                own = gs.unsqueeze(3).broadcast_to([P, NT, 4, 4])
                tt_post(g_gt[:], other, own, ALU.is_gt)
                tt(g_eq[:], other, own, ALU.is_equal)
                tt(g_eq[:].rearrange("p t g h -> p t (g h)"), g_eq[:].rearrange("p t g h -> p t (g h)"),
                   lt4[:].rearrange("p g h -> p (g h)").unsqueeze(1).broadcast_to([P, NT, 16]), ALU.mult)
                tt(g_gt[:], g_gt[:], g_eq[:], ALU.add)
                reduce(g_a[:], g_gt[:].rearrange("p t g h -> p (t g) h"))
                link(dve.tensor_scalar(g_b[:], g_a[:], 1.5, None, ALU.is_lt))
                link(dve.tensor_scalar(g_c[:], g_b[:], BIG, -BIG, ALU.mult, ALU.add))
                mquad = MB[:].rearrange("p t (g k) -> p (t g) k", k=4)
                tt(mquad, quad, g_b[:].unsqueeze(2).broadcast_to([P, NT * 4, 4]), ALU.mult)
                tt(mquad, mquad, g_c[:].unsqueeze(2).broadcast_to([P, NT * 4, 4]), ALU.add)
                for t in range(NT):
                    steps[0] += 1
                    dve.max(V8[:, t], MB[:, t]).then_inc(chain, 1)
                dve.wait_ge(chain, steps[0])
                for t in range(NT):
                    steps[0] += 1
                    dve.max_index(I8[:, t], V8[:, t], MB[:, t]).then_inc(chain, 1)
                dve.wait_ge(chain, steps[0])
                link(dve.tensor_copy(EF[:], I8[:, :, 0:TOPK]))
                oh = OH[:].rearrange("p t r e -> p (t r) e")
                tt(oh, EF[:].rearrange("p t r -> p (t r)").unsqueeze(2).broadcast_to([P, NT * TOPK, NE]),
                   free[:, 0:NE].unsqueeze(1).broadcast_to([P, NT * TOPK, NE]), ALU.is_equal)
                dve.tensor_reduce(SEL[:], OH[:].rearrange("p t r e -> p t e r"), AX_X, ALU.add).then_inc(sel_done, 1)
                tt(OT[:], OH[:], SC[:].unsqueeze(2).broadcast_to([P, NT, TOPK, NE]), ALU.mult)
                reduce(WS[:], OT[:])
                reduce(dsum[:], WS[:])
                link(dve.tensor_scalar(dsum[:], dsum[:], 1e-20, None, ALU.add))
                link(dve.reciprocal(drec[:], dsum[:]))
                tt(W4[:], WS[:], drec[:].unsqueeze(2).broadcast_to([P, NT, TOPK]), ALU.mult)
                link(dve.tensor_scalar(W4[:], W4[:], 2.5, None, ALU.mult))
                dve.wait_ge(count_ps, 1)
                link(dve.tensor_copy(TOT[:].rearrange("p t e -> p (t e)"), PS[:, 1, 0:NT * NE]))
                cur, k, n = TOT, 1, 0
                while k < NT:
                    nxt = acc[n % 2]
                    post(dve.tensor_copy(nxt[:, 0:k], cur[:, 0:k]))
                    tt(nxt[:, k:], cur[:, k:], cur[:, 0:NT - k], ALU.add)
                    cur, k, n = nxt, 2 * k, n + 1
                tt(NSK[:], cur[:, NT - 1].unsqueeze(2).broadcast_to([P, NE, B * S // SLOT]),
                   slotk[:].unsqueeze(1).broadcast_to([P, NE, B * S // SLOT]), ALU.is_gt)
                reduce(NS[:], NSK[:])
                tt_post(POS[:], cur[:], TOT[:], ALU.subtract)
                cur, k, n = NS, 1, 0
                while k < NE:
                    nxt = se[n % 2]
                    post(dve.tensor_copy(nxt[:, 0:k], cur[:, 0:k]))
                    tt(nxt[:, k:], cur[:, k:], cur[:, 0:NE - k], ALU.add)
                    cur, k, n = nxt, 2 * k, n + 1
                ends = cur
                tt(base[:], ends[:], NS[:], ALU.subtract)
                link(dve.tensor_scalar(base[:], base[:], float(SLOT), None, ALU.mult))
                tt(POS[:], POS[:], base[:].unsqueeze(1).broadcast_to([P, NT, NE]), ALU.add)
                tt(POS[:].rearrange("p t e -> p (t e)"), POS[:].rearrange("p t e -> p (t e)"), PS[:, 0, 0:NT * NE], ALU.add)
                tt(OT[:], OH[:], POS[:].unsqueeze(2).broadcast_to([P, NT, TOPK, NE]), ALU.mult)
                reduce(DEST[:], OT[:])
                link(dve.tensor_copy(DI[:], DEST[:]))
                post(dve.tensor_scalar(HII[:], DI[:], 7, None, ALU.arith_shift_right))
                link(dve.tensor_scalar(LOWI[:], DI[:], SLOT - 1, None, ALU.bitwise_and))
                post(dve.tensor_copy(HIF[:], HII[:]))
                link(dve.tensor_copy(LOW[:], LOWI[:]))
                tt_post(TOKV[:], tok[:, 0:NT].unsqueeze(2).broadcast_to([P, NT, TOPK]), LOW[:], ALU.subtract)
                link(dve.tensor_scalar(LOWI[:], DI[:], P - 1, None, ALU.bitwise_and))
                link(dve.tensor_copy(LOW[:], LOWI[:]))

                def one_hots(i, p, first=False):
                    t = HOT * i + p
                    if not first:
                        wait_apart(dve, hot_used, t - HOT + 1)
                    for hot, number, n in ((colone, HIF, NCOL), (lowhot, LOW, P)):
                        dve.tensor_tensor(hot[p], free[:, 0:n].unsqueeze(1).broadcast_to([P, TOPK, n]),
                                          number[:, t].unsqueeze(2).broadcast_to([P, TOPK, n]), ALU.is_equal).then_inc(one_hot, 1)

                for p in range(HOT):
                    one_hots(0, p, first=True)
                tt(SLE[:], ends[:].unsqueeze(1).broadcast_to([P, NSLOT, NE]),
                   free[:, 0:NSLOT].unsqueeze(2).broadcast_to([P, NSLOT, NE]), ALU.is_le)
                reduce(ESF[:], SLE[:])
                dve.tensor_scalar(ES[:], ESF[:], float(NE - 1), None, ALU.min).then_inc(es_done, 1)
                link(dve.tensor_scalar(LAST[:], ends[:, NE - 1:NE], -1.0, None, ALU.add))
                link(dve.tensor_scalar(LAST[:], LAST[:], 1, None, ALU.arith_shift_right))
                link(dve.tensor_scalar(MORE[:], LAST[:], -float(NFULL - 1), None, ALU.add))
                with dve.Fori(1, NT // HOT) as i:
                    for p in range(HOT):
                        one_hots(i, p)
                dve.wait_ge(hot_used, NT)
                tt(IDX[:].rearrange("p (s t) -> p s t", t=SLOT_T), PS[:, 2, 0:NCOL].rearrange("p (s t) -> p s t", t=SLOT_T),
                   tok[:, NT:].unsqueeze(1).broadcast_to([P, NSLOT, SLOT_T]), ALU.add)
                link(dve.tensor_copy(WPOS[:], PS[:, 2, NCOL:2 * NCOL]))
        st4.close()

        RING = 2 * SLOT_T
        NIT = NSLOT // 2

        def last_pair(eng):
            return eng.value_load(MORE[0:1, 0:1], min_val=0, max_val=NIT - NFULL) + (NFULL - 1)

        def pairs_of_slots(eng, first, last, body):
            with eng.Fori(first, NFULL - 1) as i:
                body(i)
            with eng.Fori(NFULL - 1, NIT - 1) as i:
                with eng.If(i < last):
                    body(i)

        idx = [sb(f"idx{q}", [P, 1], U32) for q in range(RING)]
        idy = [sb(f"idy{q}", [P, 1], U32) for q in range(RING)]
        xg = [sb(f"xg{q}", [P, D]) for q in range(RING)]
        yo = [sb(f"yo{q}", [P, D]) for q in range(RING)]

        def ring(name):
            return [sem(f"{name}{q}") for q in range(RING)]
        xg_in = ring("xg_in")
        idx_done, idy_done = sem("idx_done"), sem("idy_done")
        yo_done = sem("yo_done")

        def count(i, q):
            return B + 2 * i + q // 2

        add_out = [sem(f"add_out{half}") for half in range(2)]

        def next_slot(i, q):
            return i + (q + 2) // RING, (q // 2 + 1) % 2

        with nc.Block() as block_:
            @block_.sync
            def _(sp):
                def next_pair(i):
                    for w in range(2):
                        wait_apart(sp, w5_hi[w], 2 * (i + 1))
                        wait_apart(sp, w5_lo[w], 2 * (i + 1))
                        wait_apart(sp, w5_lop[w], 2 * (i + 1))
                        load_slot(sp, 2 * i + 2 + w, w)

                pairs_of_slots(sp, 0, last_pair(sp), next_pair)

            @block_.gpsimd
            def _(pool):
                def ahead(i, q, n):
                    return i + (q + n) // RING, (q + n) % RING

                def gather(i, q):
                    nc.gpsimd.tensor_copy(idx[q][:], IDX[:, bass.ds(RING * i + q, 1)]).then_inc(idx_done, 1)
                    wait_apart(pool, idx_done, RING * i + q + 1)
                    nc.gpsimd.indirect_dma_start(out=xg[q][:], out_offset=None, in_=xs_d,
                                                 in_offset=bass.IndirectOffsetOnAxis(ap=idx[q][:, 0:1], axis=0)
                                                 ).then_inc(xg_in[q], 16)

                def scatter(i, q):
                    nc.gpsimd.tensor_copy(idy[q][:], IDX[:, bass.ds(RING * i + q, 1)]).then_inc(idy_done, 1)
                    wait_apart(pool, idy_done, RING * i + q + 1)
                    wait_apart(pool, yo_done, RING * i + q + 1)
                    if q % 2 == 0:
                        for half in range(2):
                            wait_apart(pool, add_out[half], 16 * (2 * i + q // 2))
                    nc.gpsimd.indirect_dma_start(out=out, out_offset=bass.IndirectOffsetOnAxis(ap=idy[q][:, 0:1], axis=0),
                                                 in_=yo[q][:], in_offset=None, compute_op=ALU.add
                                                 ).then_inc(add_out[q % 2], 16)

                def step(i, q, first=False, last=False):
                    if not (last and q >= 1):
                        i3, q3 = ahead(i, q, 3)
                        wait_apart(pool, t4_ps[q3 % 2], count(i3, q3) - 1)
                        gather(i3, q3)
                    if not (last and q >= 2):
                        w_lo_pool(pool, *next_slot(i, q), q % 2)
                    if q % 2 == 0 and not (first and q == 0):
                        for before in (2, 1):
                            scatter(i if q >= 2 else i - 1, (q - before) % RING)

                gather(0, 0)
                gather(0, 1)
                for half in range(2):
                    w_lo_pool(pool, 0, 0, half)
                gather(0, 2)
                for q in range(RING):
                    step(0, q, first=True)

                def four_tiles(i):
                    for q in range(RING):
                        step(i, q)

                last_i = last_pair(pool)
                pairs_of_slots(pool, 1, last_i, four_tiles)
                for q in range(RING):
                    step(last_i, q, last=True)
                scatter(last_i, 2)
                scatter(last_i, 3)
                for half in range(2):
                    wait_apart(pool, add_out[half], 16 * 2 * (last_i + 1))

            @block_.scalar
            def _(act):
                def x_hi(i, q):
                    p, n = q % 2, count(i, q)
                    act.wait_ge(t4_ps[p], n + 1)
                    act.activation(x3h[p][:], bank_chunks(p), ACT.Copy).then_inc(x3_hi[p], 1)

                def silu(i, q):
                    p, n = q % 2, count(i, q)
                    act.wait_ge(gu_ps[p], n + 1)
                    act.activation(sg[p][:], PS[:, 3 + p, 0:I_FF], ACT.Silu).then_inc(silu_done[p], 1)

                def hid_hi(i, q):
                    p, n = q % 2, count(i, q)
                    act.wait_ge(t5_ps[p], n + 1)
                    act.activation(hTh[p][:], bank_chunks(5, IC), ACT.Copy).then_inc(h_hi[p], 1)

                def step(i, q, last=False):
                    if not (last and q == RING - 1):
                        x_hi(i + (q + 1) // RING, (q + 1) % RING)
                    if not (last and q >= 2):
                        w_hi_part(act, *next_slot(i, q), q % 2)
                    silu(i, q)
                    hid_hi(i, q)

                for half in range(2):
                    w_hi_part(act, 0, 0, half)
                x_hi(0, 0)

                def four_tiles(i):
                    for q in range(RING):
                        step(i, q)

                last_i = last_pair(act)
                pairs_of_slots(act, 0, last_i, four_tiles)
                for q in range(RING):
                    step(last_i, q, last=True)

            @block_.vector
            def _(dve):
                def x_lo(i, q):
                    p, n = q % 2, count(i, q)
                    dve.wait_ge(x3_hi[p], n + 1)
                    dve.tensor_tensor(x3l[p][:], bank_chunks(p), x3h[p][:].bitcast(F32), ALU.subtract).then_inc(x3_lo[p], 1)

                def hidden(i, q):
                    p, n = q % 2, count(i, q)
                    dve.wait_ge(silu_done[p], n + 1)
                    dve.scalar_tensor_tensor(out=hh[p][:], in0=PS[:, 3 + p, I_FF:2 * I_FF],
                                             scalar=WPOS[:, bass.ds(RING * i + q, 1)], in1=sg[p][:],
                                             op0=ALU.mult, op1=ALU.mult).then_inc(h_done[p], 1)

                def hid_lo(i, q):
                    p, n = q % 2, count(i, q)
                    dve.wait_ge(h_hi[p], n + 1)
                    dve.tensor_tensor(hTl[p][:], bank_chunks(5, IC), hTh[p][:].bitcast(F32), ALU.subtract).then_inc(h_lo[p], 1)

                def y_out(i, q):
                    p, n = q % 2, count(i, q)
                    if not (isinstance(i, int) and i == 0):
                        dve.wait_ge(add_out[p], 16 * (2 * i + q // 2 - 1))
                    dve.wait_ge(dn_ps[p], n + 1)
                    dve.tensor_copy(yo[q][:], PS[:, 6 + p]).then_inc(yo_done, 1)

                def step(i, q, first=False, last=False):
                    if not (last and q == RING - 1):
                        x_lo(i + (q + 1) // RING, (q + 1) % RING)
                    if not (last and q >= 2):
                        w_lo_part(dve, *next_slot(i, q), q % 2)
                    hidden(i, q)
                    if not (first and q == 0):
                        y_out(*((i, q - 1) if q else (i - 1, RING - 1)))
                    hid_lo(i, q)

                for half in range(2):
                    w_lo_part(dve, 0, 0, half)
                x_lo(0, 0)
                for q in range(RING):
                    step(0, q, first=True)

                def four_tiles(i):
                    for q in range(RING):
                        step(i, q)

                last_i = last_pair(dve)
                pairs_of_slots(dve, 1, last_i, four_tiles)
                for q in range(RING):
                    step(last_i, q, last=True)
                y_out(last_i, RING - 1)

            @block_.tensor
            def _(pe):
                def t6(i, q):
                    p, n = q % 2, count(i, q)
                    pe.wait_ge(xg_in[q], 16 * (i + 1))
                    pe.wait_ge(x3_lo[p], n)
                    for c in range(DC):
                        mm = pe.transpose(PS[:, p, c * P:(c + 1) * P], xg[q][:, c * P:(c + 1) * P], ident[:])
                    mm.then_inc(t4_ps[p], 1)

                def t7(i, q):
                    p, n = q % 2, count(i, q)
                    pe.wait_ge(h_done[p], n + 1)
                    pe.wait_ge(h_lo[1 - p], n + p)
                    for c in range(IC):
                        mm = pe.transpose(PS[:, 5, c * P:(c + 1) * P], hh[p][:, c * P:(c + 1) * P], ident[:])
                    mm.then_inc(t5_ps[p], 1)

                def down5(i, q):
                    p, n, w = q % 2, count(i, q), q // 2
                    pe.wait_ge(h_lo[p], n + 1)
                    if not (isinstance(i, int) and RING * i + q < 2):
                        pe.wait_ge(yo_done, RING * i + q - 1)
                    down(pe, p, w, dn_ps[p])

                def gu5(i, q):
                    p, n, w = q % 2, count(i, q), q // 2
                    if p == 0:
                        pe.wait_ge(w5_lo[w], 2 * (i + 1))
                        pe.wait_ge(w5_lop[w], 2 * (i + 1))
                    pe.wait_ge(x3_lo[p], n + 1)
                    pe.wait_ge(h_done[p], n)
                    gate_up(pe, p, w, gu_ps[p])

                def step(i, q, first=False, last=False):
                    if not (last and q == RING - 1):
                        t6(i + (q + 1) // RING, (q + 1) % RING)
                    gu5(i, q)
                    if not (first and q == 0):
                        down5(*((i, q - 1) if q else (i - 1, RING - 1)))
                    t7(i, q)

                t6(0, 0)
                for q in range(RING):
                    step(0, q, first=True)

                def four_tiles(i):
                    for q in range(RING):
                        step(i, q)

                last_i = last_pair(pe)
                pairs_of_slots(pe, 1, last_i, four_tiles)
                for q in range(RING):
                    step(last_i, q, last=True)
                down5(last_i, RING - 1)


_NAMES = ["x", "ctx2", "qwT", "kwT", "vwT", "owT", "q_b", "k_b", "v_b", "o_b", "ssm", "dskip", "gateT", "ebias",
          "gu_w", "dn_w", "c_ident", "c_block", "c_head", "c_lt4", "c_tri", "c_free", "c_slotk",
          "c_tok"]


def lay_out(x, ctx_2048, L0_attn_q_w, L0_attn_q_b, L0_attn_k_w, L0_attn_k_b, L0_attn_v_w, L0_attn_v_b,
            L0_attn_o_w, L0_attn_o_b, L0_xattn_ssm_kernel, L0_xattn_D, L0_ffn_gate_weight, L0_ffn_expert_bias,
            L0_ffn_gate_proj, L0_ffn_up_proj, L0_ffn_down_proj, L0_ffn_shared_gate, L0_ffn_shared_up,
            L0_ffn_shared_down):
    f = np.ascontiguousarray
    c = np.asarray(ctx_2048).reshape(B, CH, CD, DC, P)[..., ::-1].transpose(1, 4, 3, 0, 2)
    c = np.concatenate([c, c], axis=-1)
    g = np.concatenate([np.asarray(L0_ffn_gate_proj), np.asarray(L0_ffn_shared_gate)[None]])
    u = np.concatenate([np.asarray(L0_ffn_up_proj), np.asarray(L0_ffn_shared_up)[None]])
    d = np.concatenate([np.asarray(L0_ffn_down_proj), np.asarray(L0_ffn_shared_down)[None]])
    gu = np.concatenate([g, u], axis=1).transpose(0, 2, 1).reshape(NE + 1, DC, P, 2 * I_FF).transpose(0, 2, 1, 3)
    dn = d.transpose(0, 2, 1).reshape(NE + 1, IC, P, D).transpose(0, 2, 1, 3)
    p = np.arange(P)
    e = np.arange(NE)
    vals = [
        f(x), f(c), f(np.asarray(L0_attn_q_w).T), f(np.asarray(L0_attn_k_w).T), f(np.asarray(L0_attn_v_w).T),
        f(np.asarray(L0_attn_o_w).T), f(np.asarray(L0_attn_q_b).reshape(DC, P).T), f(L0_attn_k_b), f(L0_attn_v_b), f(L0_attn_o_b),
        f(L0_xattn_ssm_kernel), f(np.asarray(L0_xattn_D)[:, None]), f(np.asarray(L0_ffn_gate_weight).T),
        f(L0_ffn_expert_bias), f(gu), f(dn),
        np.eye(P, dtype=np.float32),
        (p[:, None] // HD == p[None, :] // HD).astype(np.float32),
        (p[:, None] // HD == np.arange(GPD)).astype(np.float32),
        np.broadcast_to((np.arange(4)[None, :] < np.arange(4)[:, None]).astype(np.float32), (P, 4, 4)).copy(),
        (p[:, None] < p[None, :]).astype(np.float32),
        np.broadcast_to(p.astype(np.float32), (P, P)).copy(),
        np.broadcast_to(np.arange(B * S // SLOT, dtype=np.float32) * SLOT, (P, B * S // SLOT)).copy(),
        np.concatenate([np.arange(NT)[None, :] * P + p[:, None] - B * S,
                        B * S + np.arange(SLOT_T)[None, :] * P + p[:, None]], axis=1).astype(np.float32),
    ]
    return dict(zip(_NAMES, vals))


def kernel(**inputs):
    import concourse.bacc as _bacc
    from concourse import mybir as _mybir
    from concourse.bass_utils import run_bass_kernel_spmd as _run

    nc = _bacc.Bacc("TRN2", target_bir_lowering=False, num_devices=1)
    arrays, args = {}, []
    for name, a in lay_out(**inputs).items():
        arrays[f"in_{name}"] = a
        args.append(nc.dram_tensor(f"in_{name}", a.shape, _mybir.dt.from_np(a.dtype), kind="ExternalInput").ap())
    out = nc.dram_tensor("out_y", (B * S + SLOT, D), F32, kind="ExternalOutput").ap()
    decoder_program(nc, *args, out)
    r = _run(nc, [arrays], core_ids=[0])
    return r.results[0]["out_y"][:B * S].reshape(B, S, D)
```
